# Optimizing a Trainium2 kernel written in Bass

```python
import numpy as np
import jax
import jax.numpy as jnp

def _softmax(x, axis=-1):
    return jax.nn.softmax(x, axis=axis)

def _gelu(x):
    return jax.nn.gelu(x, approximate=True)

def _silu(x):
    return jax.nn.silu(x)

def _sigmoid(x):
    return jax.nn.sigmoid(x)

def _layernorm(x, axis=-1, eps=1e-05):
    m = jnp.mean(x, axis=axis, keepdims=True)
    v = jnp.var(x, axis=axis, keepdims=True)
    return (x - m) / jnp.sqrt(v + eps)

def _scatter_add(tgt, idx, src, axis=0):
    return tgt.at[idx].add(src)

def _segment_sum(src, seg, n):
    return jax.ops.segment_sum(src, seg, n)
kernel_name = 'mk_adaln_ffn_d1_seqx_r4_637a3e'

def setup_inputs(seed: int=0):
    np.random.seed(seed)
    _w = jnp.asarray

    def _rec_inputs():
        import jax
        import jax.numpy as jnp
        _rk = jax.random.key(seed)
        x = -0.000125 + 0.9999 * jax.random.normal(jax.random.fold_in(_rk, 1), (32, 64, 256), jnp.float32)
        _lenS = 64 - jax.random.randint(jax.random.fold_in(_rk, 7), (32,), 0, max(1, 64 // 4) + 1, jnp.int32)
        _lenS2 = 64 - jax.random.randint(jax.random.fold_in(_rk, 8), (32,), 0, max(1, 64 // 4) + 1, jnp.int32)
        cond_1024 = jax.random.uniform(jax.random.fold_in(_rk, 11), (32, 256), jnp.float32, 0.0, 0.999927)
        return (x, cond_1024)
    x, cond_1024 = _rec_inputs()

    def _L0_cond_setup():
        import jax, jax.numpy as jnp
        import numpy as np
        DT = 0.001
        key = jax.random.key(seed)
        k1, k2 = jax.random.split(key)
        inputs = jax.random.normal(k1, (16, 512, 256), dtype=jnp.float32)
        initial_state = jax.random.uniform(k2, (16, 256), dtype=jnp.float32)
        return {'inputs': inputs, 'initial_state': initial_state}
    _L0_cond_all = _L0_cond_setup()
    _L0_cond_in = {k: v for k, v in _L0_cond_all.items() if k in ()}
    del _L0_cond_all

    def _L0_ffn_setup():
        import jax, jax.numpy as jnp
        import numpy as np
        HID, FFN, E, K = (256, 1024, 8, 2)
        CAP_FACTOR = 1.25
        key = jax.random.key(seed)
        k1, k2, k3, k4 = jax.random.split(key, 4)
        B, T = (4, 512)
        x = jax.random.normal(k1, (B, T, HID), dtype=jnp.float32)
        router_w = jax.random.normal(k2, (E, HID), dtype=jnp.float32) * 0.02
        w1 = jax.random.normal(k3, (E, HID, FFN), dtype=jnp.float32) * 0.02
        w2 = jax.random.normal(k4, (E, FFN, HID), dtype=jnp.float32) * 0.02
        return {'x': x, 'router_w': router_w, 'w1': w1, 'w2': w2}
    _L0_ffn_all = _L0_ffn_setup()
    _L0_ffn_in = {k: v for k, v in _L0_ffn_all.items() if k in ('router_w', 'w1', 'w2')}
    del _L0_ffn_all
    return {'x': x, 'cond_1024': cond_1024, 'L0_ffn_router_w': _L0_ffn_in['router_w'], 'L0_ffn_w1': _L0_ffn_in['w1'], 'L0_ffn_w2': _L0_ffn_in['w2']}

def reference(x, cond_1024, L0_ffn_router_w, L0_ffn_w1, L0_ffn_w2):
    import jax
    import jax.numpy as jnp

    def _L0_cond_ref(inputs, initial_state):
        import jax, jax.numpy as jnp
        import numpy as np
        DT = 0.001
        rates = jax.nn.relu(inputs) * DT
        c = initial_state[:, None, :] + jnp.cumsum(rates, axis=1)
        fl = jnp.floor(c)
        prev = jnp.concatenate([jnp.floor(initial_state)[:, None, :], fl[:, :-1, :]], axis=1)
        spikes = fl - prev
        return spikes / DT

    def _L0_ffn_ref(x, router_w, w1, w2):
        import jax, jax.numpy as jnp
        import numpy as np
        HID, FFN, E, K = (256, 1024, 8, 2)
        CAP_FACTOR = 1.25
        B, T, H = x.shape
        N = B * T
        x_flat = x.reshape(N, H)
        C = max(1, int(CAP_FACTOR * N / E * K))
        logits = x_flat @ router_w.T
        probs = jax.nn.softmax(logits, axis=-1)
        top_v, top_i = jax.lax.top_k(probs, K)
        top_v = top_v / jnp.sum(top_v, axis=-1, keepdims=True)
        out = jnp.zeros_like(x_flat)
        for k in range(K):
            eid = top_i[:, k]
            gate = top_v[:, k]
            onehot = jax.nn.one_hot(eid, E, dtype=jnp.int32)
            pos = jnp.take_along_axis(jnp.cumsum(onehot, axis=0), eid[:, None], axis=1)[:, 0] - 1
            keep = pos < C
            slot = jnp.where(keep, eid * C + pos, E * C)
            buf = jnp.zeros((E * C + 1, H), dtype=x.dtype).at[slot].add(x_flat * keep[:, None].astype(x.dtype))
            expert_in = buf[:E * C].reshape(E, C, H)
            h = jax.nn.gelu(jnp.einsum('ech,ehf->ecf', expert_in, w1), approximate=False)
            y = jnp.einsum('ecf,efh->ech', h, w2)
            tok = y.reshape(E * C, H)[jnp.minimum(slot, E * C - 1)]
            out = out + tok * (gate * keep.astype(x.dtype))[:, None]
        return out.reshape(B, T, H)
    x = x + _L0_ffn_ref(_L0_cond_ref(x, cond_1024), L0_ffn_router_w, L0_ffn_w1, L0_ffn_w2)
    return x

_drawn_inputs = setup_inputs


def setup_inputs(seed=0):
    import zlib

    import numpy as np

    out = dict(_drawn_inputs(seed))
    spreads = {}
    factors = {}
    for name, (base, spread) in spreads.items():
        noise = np.random.default_rng([zlib.crc32(name.encode()), seed]).standard_normal(out[name].shape)
        drawn = base * np.exp(spread * noise) if base else spread * noise
        out[name] = jnp.asarray(drawn.astype(out[name].dtype))
    for name, factor in factors.items():
        out[name] = (out[name] * factor).astype(out[name].dtype)
    return out
```

```python
from contextlib import ExitStack

import concourse.bass as bass
import numpy as np
from concourse import mybir

F32 = mybir.dt.float32
BF16 = mybir.dt.bfloat16
I32 = mybir.dt.int32
ALU = mybir.AluOpType
ACT = mybir.ActivationFunctionType
AX_X = mybir.AxisListType.X

P = 128
DT = np.float32(0.001)
SPIKE = float(np.float32(1.0) / DT)
TOP_K = 2
CAP_FACTOR = 1.25


def adaln_ffn_kernel(nc, x, cond, router_w, w1, w2, out):
    B, T, H = x.shape
    E, _, FFN = w1.shape
    N = B * T
    TILES = N // P
    BPT = P // T
    KC = H // P
    FC = FFN // P
    CAP = max(1, int(CAP_FACTOR * N / E * TOP_K))
    GQ = 4
    NQ = TILES // GQ

    x_tiles = x.rearrange("(j h) t c -> (h t) j c", h=BPT)
    out_tiles = out.rearrange("(j h) t c -> (h t) j c", h=BPT)

    with ExitStack() as ctx:
        def sb(name, shape, dt):
            return ctx.enter_context(nc.sbuf_tensor(name, shape, dt))

        def psum(name, shape, dt=F32):
            return ctx.enter_context(nc.psum_tensor(name, shape, dt))

        def sem(name):
            return ctx.enter_context(nc.semaphore(name))

        cum64 = sb("cum64", [P, P], F32)
        cum128 = sb("cum128", [P, P], BF16)
        ones_b = sb("ones_b", [P, P], BF16)
        ident = sb("ident", [P, P], F32)
        desc = sb("desc", [P, E], F32)
        cond_rows = sb("cond_rows", [B, H], F32)
        router_rows = sb("router_rows", [E, H], F32)
        stateT = sb("stateT", [P, KC, B], F32)
        routerT = sb("routerT", [P, KC, E], F32)

        gs_i = sb("gs_i", [P, KC, B], I32)
        gs_f = sb("gs_f", [P, KC, B], F32)
        gs_gt = sb("gs_gt", [P, KC, B], F32)
        floor_stateT = sb("floor_stateT", [P, KC, B], F32)
        g_x = sb("g_x", [P, H], F32)
        g_rate = sb("g_rate", [P, H], F32)
        g_c = sb("g_c", [P, KC, P], F32)
        g_ci = sb("g_ci", [P, KC, P], I32)
        g_cf = sb("g_cf", [P, KC, P], F32)
        g_gt = sb("g_gt", [P, KC, P], F32)
        g_fl = sb("g_fl", [P, KC, P], F32)
        g_sp = sb("g_sp", [P, KC, P], F32)
        g_xt = sb("g_xt", [P, KC, P], F32)
        g_XT = sb("g_XT", [P, KC, N], F32)
        g_e = sb("g_e", [P, E], F32)
        g_e2 = sb("g_e2", [P, E], F32)
        g_key = sb("g_key", [P, E], F32)
        g_one = sb("g_one", [P, 12], F32)
        g_oh = sb("g_oh", [P, TOP_K * E], BF16)
        g_rank = sb("g_rank", [P, TOP_K * E], F32)
        g_seen = sb("g_seen", [P, TOP_K * E], F32)
        g_kept = sb("g_kept", [P, TOP_K * E], F32)
        g_tmp = sb("g_tmp", [P, E], F32)
        g_gates = sb("g_gates", [P, TILES * E], F32)
        g_gcol = sb("g_gcol", [P, GQ], F32)
        g_w1 = sb("g_w1", [P, 2, KC, FFN], F32)
        g_w2 = sb("g_w2", [P, 2, FC, H], F32)
        g_h = sb("g_h", [P, FC, GQ * P], F32)
        g_acc = sb("g_acc", [P, TILES, H], F32)

        bank = [psum(f"bank{i}", [P, 512]) for i in range(8)]

        consts = sem("consts")
        masks = sem("masks")
        small_in = sem("small_in")
        turned = sem("turned")
        turned_out = sem("turned_out")
        gx_in = sem("gx_in")
        g_vec = sem("g_vec")
        g_rates = sem("g_rates")
        g_cums = sem("g_cums")
        g_xts = sem("g_xts")
        g_logits = sem("g_logits")
        g_max = sem("g_max")
        g_exps = sem("g_exps")
        g_hot = sem("g_hot")
        g_ranks = sem("g_ranks")
        g_routed = sem("g_routed")
        w_in = [sem("w_in0"), sem("w_in1")]
        acc_in = sem("acc_in")
        h_mm = sem("h_mm")
        h_act = sem("h_act")
        y_mm = sem("y_mm")
        y_add = sem("y_add")
        out_done = sem("out_done")
        block = ctx.enter_context(nc.Block())

        csum = bank[0][:, 0:KC * P].rearrange("p (k n) -> p k n", k=KC)
        logit = bank[1][:, 0:E]
        rank_ps = bank[2][:, 0:TOP_K * E]
        total_ps = bank[3][:, 0:TOP_K * E]
        V = 28

        @block.sync
        def _(sp):
            sp.dma_start(cond_rows[:, :], cond).then_inc(small_in, 16)
            sp.dma_start(router_rows[:, :], router_w).then_inc(small_in, 16)
            sp.dma_start(g_acc[:, :, :], x_tiles).then_inc(acc_in, 16)
            with sp.Fori(0, TILES) as j:
                sp.wait_ge(g_rates, j + 1)
                sp.dma_start(g_x[:, :], x_tiles[:, bass.ds(j, 1), :].rearrange("p a c -> p (a c)")).then_inc(gx_in, 16)
            with sp.Fori(0, E // 2) as pair:
                for side in range(2):
                    e = pair * 2 + side
                    sp.wait_ge(y_mm, pair * (2 * NQ) + 1)
                    sp.dma_start(g_w1[:, side, :, :], w1[bass.ds(e, 1), :, :].rearrange("e (k p) f -> p (e k) f", p=P)).then_inc(w_in[side], 16)
                    sp.dma_start(g_w2[:, side, :, :], w2[bass.ds(e, 1), :, :].rearrange("e (k p) c -> p (e k) c", p=P)).then_inc(w_in[side], 16)
            sp.wait_ge(y_add, E * NQ * GQ + 1)
            sp.dma_start(out_tiles, g_acc[:, :, :]).then_inc(out_done, 16)
            sp.wait_ge(out_done, 16)

        @block.gpsimd
        def _(pool):
            nc.gpsimd.memset(cum64[:, :], 1.0).then_inc(consts, 1)
            nc.gpsimd.memset(cum128[:, :], 1.0).then_inc(consts, 1)
            nc.gpsimd.memset(ones_b[:, :], 1.0).then_inc(consts, 1)
            nc.gpsimd.memset(ident[:, :], 0.0).then_inc(consts, 1)
            nc.gpsimd.iota(desc[:, :], [[-1, E]], base=E, channel_multiplier=0,
                           allow_small_or_imprecise_dtypes=True).then_inc(masks, 1)
            pool.wait_ge(consts, 4)
            for m in (cum64, cum128):
                nc.gpsimd.affine_select(out=m[:, :], in_=m[:, :], compare_op=ALU.is_ge, fill=0.0, base=0,
                                        pattern=[[1, P]], channel_multiplier=-1).then_inc(consts, 1)
            nc.gpsimd.affine_select(out=ident[:, :], in_=ident[:, :], compare_op=ALU.not_equal, fill=1.0, base=0,
                                    pattern=[[-1, P]], channel_multiplier=1).then_inc(masks, 1)
            pool.wait_ge(consts, 6)
            nc.gpsimd.memset(cum64[0:T, T:P], 0.0).then_inc(masks, 1)

        @block.tensor
        def _(pe):
            pe.sem_inc(y_mm, 1)
            pe.wait_ge(masks, 3)
            pe.wait_ge(small_in, 32)
            for k in range(KC):
                nc.tensor.transpose(bank[0][:, k * B:(k + 1) * B], cond_rows[:, k * P:(k + 1) * P], ident[0:B, 0:B])
            for k in range(KC):
                last = nc.tensor.transpose(bank[1][:, k * E:(k + 1) * E], router_rows[:, k * P:(k + 1) * P], ident[0:E, 0:E])
            last.then_inc(turned, 1)
            pe.wait_ge(turned_out, 2)
            with pe.Fori(0, TILES) as j:
                pe.wait_ge(g_rates, j + 2)
                for k in range(KC):
                    mm = nc.tensor.matmul(csum[:, k, :], g_rate[:, k * P:(k + 1) * P], cum64[:, :], start=True, stop=True)
                mm.then_inc(g_cums, 1)
                pe.wait_ge(g_xts, j + 1)
                for k in range(KC):
                    mm = nc.tensor.matmul(logit, g_xt[:, k, :], routerT[:, k, :], start=(k == 0), stop=(k == KC - 1))
                mm.then_inc(g_logits, 1)
                pe.wait_ge(g_hot, j + 1)
                nc.tensor.matmul(rank_ps, cum128[:, :], g_oh[:, :], start=True, stop=True)
                nc.tensor.matmul(total_ps, ones_b[:, :], g_oh[:, :], start=True, stop=True).then_inc(g_ranks, 1)
            pe.wait_ge(g_routed, 1)
            with pe.Fori(0, E // 2) as pair:
                for side in range(2):
                    with pe.Fori(0, NQ) as q:
                        step = (pair * 2 + side) * NQ + q
                        pe.wait_ge(w_in[side], pair * 32 + 32)
                        for f in range(FC):
                            if f < 2:
                                pe.wait_ge(h_act, step * FC + 1)
                            else:
                                pe.wait_ge(h_act, step * FC + f)
                            for k in range(KC):
                                mm = nc.tensor.matmul(bank[f % 2][:, 0:GQ * P], g_w1[:, side, k, f * P:(f + 1) * P],
                                                      g_XT[:, k, bass.ds(q * (GQ * P), GQ * P)],
                                                      start=(k == 0), stop=(k == KC - 1))
                            mm.then_inc(h_mm, 1)
                        pe.wait_ge(h_act, step * FC + FC + 1)
                        pe.wait_ge(y_add, step * GQ + 1)
                        for s in range(GQ):
                            for f in range(FC):
                                mm = nc.tensor.matmul(bank[2 + s][:, 0:H], g_h[:, f, s * P:(s + 1) * P], g_w2[:, side, f, :],
                                                      start=(f == 0), stop=(f == FC - 1))
                        mm.then_inc(y_mm, 1)

        @block.scalar
        def _(act):
            act.sem_inc(h_act, 1)
            with act.Fori(0, TILES) as j:
                act.wait_ge(g_max, j + 1)
                nc.scalar.activation(g_e[:, :], logit, ACT.Exp, bias=g_one[:, 1:2]).then_inc(g_exps, 1)
            with act.Fori(0, E * NQ) as step:
                for f in range(FC):
                    act.wait_ge(h_mm, step * FC + f + 1)
                    if f == 0:
                        act.wait_ge(y_mm, step + 1)
                    nc.scalar.activation(g_h[:, f, :], bank[f % 2][:, 0:GQ * P], ACT.Gelu).then_inc(h_act, 1)

        @block.vector
        def _(dve):
            dve.sem_inc(g_rates, 1)
            dve.sem_inc(y_add, 1)
            dve.wait_ge(turned, 1)
            nc.vector.tensor_copy(stateT[:, :, :], bank[0][:, 0:KC * B].rearrange("p (k b) -> p k b", k=KC)).then_inc(turned_out, 1)
            nc.vector.tensor_copy(routerT[:, :, :], bank[1][:, 0:KC * E].rearrange("p (k e) -> p k e", k=KC)).then_inc(turned_out, 1)
            dve.wait_ge(turned_out, 2)
            nc.vector.tensor_copy(gs_i[:, :, :], stateT[:, :, :]).then_inc(turned_out, 1)
            dve.wait_ge(turned_out, 3)
            nc.vector.tensor_copy(gs_f[:, :, :], gs_i[:, :, :]).then_inc(turned_out, 1)
            dve.wait_ge(turned_out, 4)
            nc.vector.tensor_tensor(gs_gt[:, :, :], gs_f[:, :, :], stateT[:, :, :], ALU.is_gt).then_inc(turned_out, 1)
            dve.wait_ge(turned_out, 5)
            nc.vector.tensor_tensor(floor_stateT[:, :, :], gs_f[:, :, :], gs_gt[:, :, :], ALU.subtract).then_inc(turned_out, 1)
            nc.vector.memset(g_seen[:, :], 0.0).then_inc(turned_out, 1)
            dve.wait_ge(turned_out, 7)
            dve.wait_ge(masks, 3)
            with dve.Fori(0, TILES) as j:
                done = [0]

                def link(ins):
                    done[0] += 1
                    ins.then_inc(g_vec, 1)
                    dve.wait_ge(g_vec, j * V + done[0])

                one = lambda n: g_one[:, n:n + 1]
                dve.wait_ge(gx_in, j * 16 + 16)
                nc.vector.tensor_scalar(g_rate[:, :], g_x[:, :], 0.0, float(DT), ALU.max, ALU.mult).then_inc(g_rates, 1)
                dve.wait_ge(g_cums, j + 1)
                for k in range(KC):
                    link(nc.vector.tensor_tensor(
                        g_c[:, k, :].rearrange("p (b t) -> p b t", b=BPT), csum[:, k, :].rearrange("p (b t) -> p b t", b=BPT),
                        stateT[:, k, bass.ds(j * BPT, BPT)].unsqueeze(2).to_broadcast([P, BPT, T]), ALU.add))
                link(nc.vector.tensor_copy(g_ci[:, :, :], g_c[:, :, :]))
                link(nc.vector.tensor_copy(g_cf[:, :, :], g_ci[:, :, :]))
                link(nc.vector.tensor_tensor(g_gt[:, :, :], g_cf[:, :, :], g_c[:, :, :], ALU.is_gt))
                link(nc.vector.tensor_tensor(g_fl[:, :, :], g_cf[:, :, :], g_gt[:, :, :], ALU.subtract))
                fl = g_fl[:, :, :].rearrange("p k (b t) -> p (k b) t", b=BPT)
                spk = g_sp[:, :, :].rearrange("p k (b t) -> p (k b) t", b=BPT)
                link(nc.vector.tensor_tensor(spk[:, :, 1:T], fl[:, :, 1:T], fl[:, :, 0:T - 1], ALU.subtract))
                for k in range(KC):
                    link(nc.vector.tensor_tensor(spk[:, k * BPT:(k + 1) * BPT, 0], fl[:, k * BPT:(k + 1) * BPT, 0],
                                                 floor_stateT[:, k, bass.ds(j * BPT, BPT)], ALU.subtract))
                nc.vector.tensor_scalar(g_xt[:, :, :], g_sp[:, :, :], SPIKE, None, ALU.mult).then_inc(g_xts, 1)
                dve.wait_ge(g_xts, j + 1)
                link(nc.vector.tensor_copy(g_XT[:, :, bass.ds(j * P, P)], g_xt[:, :, :]))
                dve.wait_ge(g_logits, j + 1)
                link(nc.vector.tensor_reduce(one(0), logit, AX_X, ALU.max))
                nc.vector.tensor_scalar(one(1), one(0), -1.0, None, ALU.mult).then_inc(g_max, 1)
                dve.wait_ge(g_exps, j + 1)
                link(nc.vector.tensor_reduce(one(2), g_e[:, :], AX_X, ALU.max))
                link(nc.vector.scalar_tensor_tensor(g_key[:, :], g_e[:, :], one(2), desc[:, :], ALU.is_equal, ALU.mult))
                link(nc.vector.tensor_reduce(one(3), g_key[:, :], AX_X, ALU.max))
                link(nc.vector.tensor_scalar(g_oh[:, 0:E], desc[:, :], one(3), None, ALU.is_equal))
                link(nc.vector.scalar_tensor_tensor(g_e2[:, :], g_oh[:, 0:E], -2.0, g_e[:, :], ALU.mult, ALU.add))
                link(nc.vector.tensor_reduce(one(4), g_e2[:, :], AX_X, ALU.max))
                link(nc.vector.scalar_tensor_tensor(g_key[:, :], g_e2[:, :], one(4), desc[:, :], ALU.is_equal, ALU.mult))
                link(nc.vector.tensor_reduce(one(5), g_key[:, :], AX_X, ALU.max))
                nc.vector.tensor_scalar(g_oh[:, E:2 * E], desc[:, :], one(5), None, ALU.is_equal).then_inc(g_hot, 1)
                link(nc.vector.tensor_tensor(one(6), one(2), one(4), ALU.add))
                link(nc.vector.reciprocal(one(7), one(6)))
                link(nc.vector.tensor_tensor(one(8), one(2), one(7), ALU.mult))
                link(nc.vector.tensor_tensor(one(9), one(4), one(7), ALU.mult))
                dve.wait_ge(g_ranks, j + 1)
                dve.wait_ge(g_hot, j + 1)
                link(nc.vector.tensor_tensor(g_rank[:, :], rank_ps, g_seen[:, :], ALU.add))
                link(nc.vector.tensor_tensor(g_seen[:, :], total_ps, g_seen[:, :], ALU.add))
                link(nc.vector.scalar_tensor_tensor(g_kept[:, :], g_rank[:, :], float(CAP), g_oh[:, :], ALU.is_le, ALU.mult))
                link(nc.vector.tensor_scalar(g_tmp[:, :], g_kept[:, 0:E], one(8), None, ALU.mult))
                link(nc.vector.scalar_tensor_tensor(g_gates[:, bass.ds(j * E, E)], g_kept[:, E:2 * E], one(9), g_tmp[:, :], ALU.mult, ALU.add))
                assert done[0] == V, done
            nc.vector.tensor_copy(g_one[:, 10:11], g_one[:, 9:10]).then_inc(g_routed, 1)
            dve.wait_ge(acc_in, 16)
            gates3 = g_gates[:, :].rearrange("p (j e) -> p j e", e=E)
            with dve.Fori(0, E) as e:
                with dve.Fori(0, NQ) as q:
                    step = e * NQ + q
                    dve.wait_ge(y_add, step * GQ + 1)
                    nc.vector.tensor_copy(g_gcol[:, :], gates3[:, bass.ds(q * GQ, GQ), bass.ds(e, 1)].rearrange("p a b -> p (a b)")).then_inc(g_routed, 1)
                    dve.wait_ge(g_routed, step + 2)
                    dve.wait_ge(y_mm, step + 2)
                    for s in range(GQ):
                        a = g_acc[:, bass.ds(q * GQ + s, 1), :].rearrange("p a c -> p (a c)")
                        nc.vector.scalar_tensor_tensor(a, bank[2 + s][:, 0:H], g_gcol[:, s:s + 1], a, ALU.mult, ALU.add).then_inc(y_add, 1)


_INS = ["x", "cond_1024", "L0_ffn_router_w", "L0_ffn_w1", "L0_ffn_w2"]
_OUTS = [((32, 64, 256), "float32")]


def kernel(**inputs):
    import numpy as _np
    import concourse.bacc as _bacc
    from concourse import mybir as _mybir
    from concourse.bass_utils import run_bass_kernel_spmd as _run

    nc = _bacc.Bacc("TRN2", target_bir_lowering=False, num_devices=1)
    arrays, args = {}, []
    for name in _INS:
        a = _np.ascontiguousarray(inputs[name])
        arrays[f"in_{name}_dram"] = a
        args.append(nc.dram_tensor(f"in_{name}_dram", a.shape, _mybir.dt.from_np(a.dtype), kind="ExternalInput").ap())
    for i, (shape, dtype) in enumerate(_OUTS):
        dt = _mybir.dt.from_np(_np.dtype(dtype))
        args.append(nc.dram_tensor(f"out_{i}_dram", shape, dt, kind="ExternalOutput").ap())
    adaln_ffn_kernel(nc, *args)
    r = _run(nc, [arrays], core_ids=[0])
    return r.results[0]["out_0_dram"]
```

```python
from contextlib import ExitStack

import concourse.bass as bass
import numpy as np
from concourse import mybir

F32 = mybir.dt.float32
BF16 = mybir.dt.bfloat16
I32 = mybir.dt.int32
U32 = mybir.dt.uint32
ALU = mybir.AluOpType
ACT = mybir.ActivationFunctionType
AX_X = mybir.AxisListType.X

P = 128
DT = np.float32(0.001)
SPIKE = float(np.float32(1.0) / DT)
TOP_K = 2
CAP_FACTOR = 1.25
HALF_ULP = 2.0 ** -25
RUN_MAX = 0.49
FAR = 4096.0


def adaln_ffn_kernel(nc, x, cond, router_w, w1, w2, out):
    B, T, H = x.shape
    E, _, FFN = w1.shape
    N = B * T
    TILES = N // P
    BPT = P // T
    KC = H // P
    FC = FFN // P
    CAP = max(1, int(CAP_FACTOR * N / E * TOP_K))
    ST = 2
    SLOTS = ST * P
    PAIRS = 80
    EVENTS = P
    JM = 8
    IDLE_TILES = -(-(SLOTS + PAIRS) // P)
    GROUPS = [(0, 1), (1, 3), (4, 4)]
    XG = TILES // 2
    GW = 2 * H

    x_tiles = x.rearrange("(j h) t c -> (h t) j c", h=BPT)
    out_tiles = out.rearrange("(j h) t c -> (h t) j c", h=BPT)
    out_rows = out.rearrange("b t c -> (b t) c")
    w1_rows = w1.rearrange("e h f -> (e h) f")

    with ExitStack() as ctx:
        def sb(name, shape, dt=F32):
            return ctx.enter_context(nc.sbuf_tensor(name, shape, dt))

        def psum(name, shape, dt=F32):
            return ctx.enter_context(nc.psum_tensor(name, shape, dt))

        def sem(name):
            return ctx.enter_context(nc.semaphore(name))

        cum_seq = sb("cum_seq", [P, P])
        cum_tile = sb("cum_tile", [P, P], BF16)
        step_seq = sb("step_seq", [P, P], BF16)
        ones_b = sb("ones_b", [P, P], BF16)
        ident = sb("ident", [P, P])
        ident3 = sb("ident3", [3 * B, B], BF16)
        slot1 = sb("slot1", [P, SLOTS], BF16)
        place = sb("place", [P, EVENTS], BF16)
        eight = sb("eight", [P, JM])
        part = sb("part", [P, 1])
        slot_no = sb("slot_no", [P, ST])
        token1 = sb("token1", [P, IDLE_TILES])
        first_two = sb("first_two", [P, TOP_K * E])
        row_base = sb("row_base", [P, E])
        desc = sb("desc", [P, E])
        carry = sb("carry", [P, TILES])

        cond3 = sb("cond3", [3 * B, H])
        theta = sb("theta", [3 * B, H])
        theta_r = sb("theta_r", [3 * B, H])
        theta_hi = sb("theta_hi", [3 * B, H], BF16)
        theta_mid = sb("theta_mid", [3 * B, H], BF16)
        theta3 = sb("theta3", [3 * B, H], BF16)
        in_range = sb("in_range", [3 * B, H])
        spread = sb("spread", [3 * B, B, T], BF16)
        router_rows = sb("router_rows", [E, H])
        routerT = sb("routerT", [P, KC, E])
        x_sb = sb("x_sb", [P, TILES, H])
        RING = 4
        rate = sb("rate", [P, RING, 2, H])
        theta_tok = sb("theta_tok", [P, TILES, H])
        XW = H + 4
        floors = sb("floors", [P, RING, 2, H], BF16)
        spikes = sb("spikes", [P, TILES, XW], BF16)
        over = sb("over", [P, GW], BF16)
        floor_sum = sb("floor_sum", [P, TILES], BF16)
        active = sb("active", [P, TILES], BF16)
        before = sb("before", [P, TILES + 1])
        rank_t = sb("rank_t", [P, TILES])
        slot_of = sb("slot_of", [P, TILES])
        idle_a = sb("idle_a", [P, IDLE_TILES])
        idle_b = sb("idle_b", [P, IDLE_TILES])
        idle_rank = sb("idle_rank", [P, IDLE_TILES])
        to_slot = sb("to_slot", [P, TILES, SLOTS], BF16)
        to_idle = sb("to_idle", [P, IDLE_TILES, PAIRS], BF16)
        spikesT = sb("spikesT", [P, KC, SLOTS])
        slot_info = sb("slot_info", [P, ST, 3])
        keyed = sb("keyed", [P, ST, H])
        chan = sb("chan", [P, ST, JM])
        chan_b = sb("chan_b", [P, ST, JM], BF16)
        chan_hit = sb("chan_hit", [P, ST, JM])
        hits = sb("hits", [P, ST])
        top_l = sb("top_l", [P, ST])
        shifted = sb("shifted", [P, ST, E])
        expo = sb("expo", [P, ST, E])
        best = sb("best", [P, ST, JM])
        best_at = sb("best_at", [P, ST, JM], U32)
        best_f = sb("best_f", [P, ST, TOP_K])
        chosen = sb("chosen", [P, ST, TOP_K * E], BF16)
        token_no = sb("token_no", [P, ST])
        inactive = sb("inactive", [P, ST])
        unused = sb("unused", [P, ST])
        base = sb("base", [P, ST, TOP_K * E])
        rank_s = sb("rank_s", [P, ST, TOP_K * E])
        kept = sb("kept", [P, ST, TOP_K * E])
        routed = sb("routed", [P, ST, 2 * E], BF16)
        pair_at = sb("pair_at", [P, ST, E])
        places = sb("places", [P, ST, 2 * E])
        ev_start = sb("ev_start", [P, ST, E])
        ev_start_b = sb("ev_start_b", [P, ST, E], BF16)
        top_sum = sb("top_sum", [P, ST])
        top_inv = sb("top_inv", [P, ST])
        gate1 = sb("gate1", [P, ST])
        gate2 = sb("gate2", [P, ST])
        gates_a = sb("gates_a", [P, ST, E])
        gates_b = sb("gates_b", [P, ST, E])
        gates = sb("gates", [P, ST, E])
        gates_r = sb("gates_r", [P, ST, E])
        pair_info = sb("pair_info", [P, ST, 6, E], BF16)
        to_pair = sb("to_pair", [P, ST, E, PAIRS], BF16)
        from_start = sb("from_start", [P, ST, E, EVENTS], BF16)
        from_end = sb("from_end", [P, ST, E, EVENTS], BF16)
        ev_maps = [sb(f"ev_maps{n}", [P, ne * (PAIRS + JM + 1)]) for n, (_, ne) in enumerate(GROUPS)]
        nth = sb("nth", [P, E])
        nth_hit = sb("nth_hit", [P, E, JM])
        nth_chan = sb("nth_chan", [P, E, JM])
        ev_chan = sb("ev_chan", [P, E])
        ev_far = sb("ev_far", [P, E])
        ev_row = sb("ev_row", [P, E])
        w1_index = sb("w1_index", [P, E], I32)
        w1_got = sb("w1_got", [P, E, FFN])
        w2_sb = sb("w2_sb", [P, E, FC, H])
        hT = sb("hT", [P, 2, FC, PAIRS])
        yT = sb("yT", [P, 2, KC, PAIRS])
        y = sb("y", [PAIRS, 3, H])
        pairs = sb("pairs", [PAIRS, E, 6])
        idle_row = sb("idle_row", [PAIRS, 1])
        idle_in = sb("idle_in", [PAIRS, 2])
        pair_a = sb("pair_a", [PAIRS, E])
        pair_gate = sb("pair_gate", [PAIRS, E])
        pair_free = sb("pair_free", [PAIRS, E])
        pair_row = sb("pair_row", [PAIRS, E])
        out_index = sb("out_index", [PAIRS, E], I32)
        NV = 8 + 1 + ST + 1 + 2 * ST * E
        faults = sb("faults", [P, NV])
        fine = sb("fine", [P, NV])
        fine_sum = sb("fine_sum", [P, 1])
        fine_all = sb("fine_all", [1, 1])
        verdict = sb("verdict", [1, 1], I32)
        run_max = sb("run_max", [P, 1])
        warm = sb("warm", [P, 3])
        carry_f = sb("carry_f", [P, 1])

        gs_i = sb("gs_i", [P, KC, B], I32)
        gs_f = sb("gs_f", [P, KC, B])
        gs_gt = sb("gs_gt", [P, KC, B])
        stateT = sb("stateT", [P, KC, B])
        floor_stateT = sb("floor_stateT", [P, KC, B])
        g_ci = sb("g_ci", [P, KC, P], I32)
        spare = rate[:, :, :, :].rearrange("p r a c -> p (r a) c")
        g_x, g_rate = spare[:, 0, :], spare[:, 1, :]
        g_c, g_cf, g_gt, g_fl, g_sp, g_xt = (spare[:, 2 + i, :].rearrange("p (k n) -> p k n", k=KC) for i in range(6))
        g_e = sb("g_e", [P, E])
        g_e2 = sb("g_e2", [P, E])
        g_key = sb("g_key", [P, E])
        g_one = sb("g_one", [P, 12])
        g_oh = sb("g_oh", [P, TOP_K * E], BF16)
        g_rank = sb("g_rank", [P, TOP_K * E])
        g_seen = sb("g_seen", [P, TOP_K * E])
        g_kept = sb("g_kept", [P, TOP_K * E])
        g_tmp = sb("g_tmp", [P, E])
        g_gates = sb("g_gates", [P, TILES * E])
        GQ = 4
        NQ = TILES // GQ
        V = 28
        g_gcol = sb("g_gcol", [P, GQ])
        g_XT = theta_tok[:, :, :].rearrange("p j c -> p (j c)").rearrange("p (k n) -> p k n", k=KC)
        w2_flat = w2_sb[:, :, :, :].rearrange("p e f c -> p (e f c)")
        size = 2 * KC * FFN
        g_w1 = w2_flat[:, 0:size].rearrange("p (s k f) -> p s k f", s=2, k=KC)
        g_w2 = w2_flat[:, size:2 * size].rearrange("p (s f c) -> p s f c", s=2, f=FC)
        g_h = w2_flat[:, 2 * size:2 * size + FC * GQ * P].rearrange("p (f n) -> p f n", f=FC)
        g_acc = x_sb

        bank = [psum(f"bank{i}", [P, 512]) for i in range(8)]

        consts = sem("consts")
        masks = sem("masks")
        cleared = sem("cleared")
        small_in = sem("small_in")
        x_in = [sem(f"x_in{i}") for i in range(4)]
        w2_in = [sem(f"w2_in{i}") for i in range(E)]
        copied = sem("copied")
        vec = sem("vec")
        theta_set = sem("theta_set")
        thetas = sem("thetas")
        theta_out = sem("theta_out")
        router_t = sem("router_t")
        router_out = sem("router_out")
        rates = sem("rates")
        cums = sem("cums")
        checked = sem("checked")
        floored = sem("floored")
        summed = sem("summed")
        diffs = sem("diffs")
        spikes_out = sem("spikes_out")
        counts = sem("counts")
        act_set = sem("act_set")
        info_set = sem("info_set")
        prefixed = sem("prefixed")
        slotted = sem("slotted")
        idle_set = sem("idle_set")
        compactT = sem("compactT")
        spikesT_out = sem("spikesT_out")
        compact = sem("compact")
        idled = sem("idled")
        keyed_set = sem("keyed_set")
        logits = sem("logits")
        shift_set = sem("shift_set")
        exps = sem("exps")
        chose = sem("chose")
        ranked = sem("ranked")
        routes = sem("routes")
        placed = sem("placed")
        maps_set = sem("maps_set")
        info_set2 = sem("info_set2")
        mapped = sem("mapped")
        map_out = sem("map_out")
        indexed = sem("indexed")
        pair_mm = sem("pair_mm")
        paired = sem("paired")
        w1_in = [sem(f"w1_in{i}") for i in range(E)]
        h_ready = sem("h_ready")
        h_done = sem("h_done")
        yT_ready = sem("yT_ready")
        yT_out = sem("yT_out")
        y_turned = sem("y_turned")
        y_set = sem("y_set")
        added = sem("added")
        summed_up = sem("summed_up")
        verdict_mm = sem("verdict_mm")
        verdict_set = sem("verdict_set")

        turned = sem("turned")
        turned_out = sem("turned_out")
        gx_in = sem("gx_in")
        g_vec = sem("g_vec")
        g_rates = sem("g_rates")
        g_cums = sem("g_cums")
        g_xts = sem("g_xts")
        g_logits = sem("g_logits")
        g_max = sem("g_max")
        g_exps = sem("g_exps")
        g_hot = sem("g_hot")
        g_ranks = sem("g_ranks")
        g_routed = sem("g_routed")
        w_in = [sem("w_in0"), sem("w_in1")]
        h_mm = sem("h_mm")
        h_act = sem("h_act")
        y_mm = sem("y_mm")
        y_add = sem("y_add")
        out_done = sem("out_done")

        CUM = [bank[i] for i in range(3)]
        DIF = [bank[3 + i] for i in range(3)]
        count_ps = bank[6][:, 0:TILES]
        within_ps = bank[7][:, 32:32 + TILES]
        total_ps_s = bank[7][:, 64:64 + TILES]
        slotsT_ps = [bank[k][:, 0:SLOTS] for k in range(KC)]
        slots_ps = [bank[2 + t][:, 0:H + 3] for t in range(ST)]
        logit_s = bank[4][:, 0:ST * E].rearrange("p (t e) -> p t e", t=ST)
        rank_ps_s = bank[5][:, 0:ST * 2 * E].rearrange("p (t e) -> p t e", t=ST)
        place_ps = bank[5][:, 64:64 + ST * 2 * E].rearrange("p (t e) -> p t e", t=ST)
        idle_ps = bank[7][0:PAIRS, 0:2]
        pair_ps = bank[7][0:PAIRS, 32:32 + 6 * E].rearrange("p (e i) -> p e i", e=E)
        verdict_ps = bank[0][0:1, 0:1]
        MAP = [bank[i % 2] for i in range(len(GROUPS))]
        HID = [[bank[2], bank[3]], [bank[4], bank[5]]]
        CH = FC // 2

        YT = [bank[6], bank[0]]
        YR = [bank[7][0:PAIRS, 256:256 + H], bank[1][0:PAIRS, 256:256 + H]]

        def maps_of(g, src=None):
            e0, ne = GROUPS[g]
            flat = MAP[g] if src is None else src[g]
            size = ne * PAIRS
            return (flat[:, 0:size].rearrange("p (e n) -> p e n", e=ne),
                    flat[:, size:size + ne * (JM + 1)].rearrange("p (e n) -> p e n", e=ne))

        bias_set = sem("bias_set")
        warmed = sem("warmed")

        csum = bank[0][:, 0:KC * P].rearrange("p (k n) -> p k n", k=KC)
        logit = bank[1][:, 0:E]
        rank_ps = bank[2][:, 0:TOP_K * E]
        total_ps = bank[3][:, 0:TOP_K * E]

        block = ctx.enter_context(nc.Block())

        @block.sync
        def _(sp):
            quarter = TILES // 4
            for i in range(4):
                sp.dma_start(x_sb[:, i * quarter:(i + 1) * quarter, :],
                             x_tiles[:, i * quarter:(i + 1) * quarter, :]).then_inc(x_in[i], 16)
            for e in range(E):
                sp.dma_start(w2_sb[:, e, :, :], w2[e].rearrange("(f p) c -> p f c", p=P)).then_inc(w2_in[e], 16)
                if e == 1:
                    for i in range(4):
                        sp.wait_ge(x_in[i], 16)
                    sp.dma_start(out_tiles, x_sb[:, :, :]).then_inc(copied, 16)
            sp.wait_ge(copied, 16)
            sp.wait_ge(added, 16 * E)

            sp.wait_ge(verdict_set, 1)
            with sp.If(sp.value_load(verdict[0:1, 0:1]) != P * NV):
                with sp.Fori(0, TILES) as j:
                    sp.wait_ge(g_rates, j + 1)
                    sp.dma_start(g_x[:, :], x_tiles[:, bass.ds(j, 1), :].rearrange("p a c -> p (a c)")).then_inc(gx_in, 16)
                with sp.Fori(0, E // 2) as pair:
                    for side in range(2):
                        e = pair * 2 + side
                        sp.wait_ge(y_mm, pair * (2 * NQ) + 1)
                        sp.dma_start(g_w1[:, side, :, :], w1[bass.ds(e, 1), :, :].rearrange("e (k p) f -> p (e k) f", p=P)).then_inc(w_in[side], 16)
                        sp.dma_start(g_w2[:, side, :, :], w2[bass.ds(e, 1), :, :].rearrange("e (k p) c -> p (e k) c", p=P)).then_inc(w_in[side], 16)
                sp.wait_ge(y_add, E * NQ * GQ + 1)
                sp.dma_start(out_tiles, g_acc[:, :, :]).then_inc(out_done, 16)
                sp.wait_ge(out_done, 16)

        @block.gpsimd
        def _(pool):
            g = nc.gpsimd
            g.memset(ident3[:, :], 0.0).then_inc(consts, 1)
            g.memset(cum_seq[:, :], 1.0).then_inc(consts, 1)
            g.memset(step_seq[:, :], 0.0).then_inc(consts, 1)
            g.memset(cum_tile[:, :], 1.0).then_inc(consts, 1)
            g.memset(ident[:, :], 0.0).then_inc(consts, 1)
            pool.wait_ge(consts, 5)
            for i in range(3):
                g.affine_select(out=ident3[i * B:(i + 1) * B, :], in_=ident3[i * B:(i + 1) * B, :],
                                compare_op=ALU.not_equal, fill=1.0, base=0, pattern=[[-1, B]],
                                channel_multiplier=1).then_inc(masks, 1)
            pool.wait_ge(masks, 3)
            for m in (cum_seq, cum_tile):
                g.affine_select(out=m[:, :], in_=m[:, :], compare_op=ALU.is_ge, fill=0.0, base=0,
                                pattern=[[1, P]], channel_multiplier=-1).then_inc(consts, 1)
            g.affine_select(out=step_seq[:, :], in_=step_seq[:, :], compare_op=ALU.not_equal, fill=1.0, base=0,
                            pattern=[[-1, P]], channel_multiplier=1).then_inc(consts, 1)
            pool.wait_ge(consts, 8)
            g.memset(cum_seq[0:T, T:P], 0.0).then_inc(masks, 1)
            g.affine_select(out=step_seq[:, :], in_=step_seq[:, :], compare_op=ALU.not_equal, fill=-1.0, base=1,
                            pattern=[[-1, P]], channel_multiplier=1).then_inc(consts, 1)
            pool.wait_ge(consts, 9)
            g.memset(step_seq[0:T, T:P], 0.0).then_inc(masks, 1)
            g.affine_select(out=ident[:, :], in_=ident[:, :], compare_op=ALU.not_equal, fill=1.0, base=0,
                            pattern=[[-1, P]], channel_multiplier=1).then_inc(masks, 1)

            def count(out, pattern, base=0, step=0):
                return g.iota(out, pattern, base=base, channel_multiplier=step,
                              allow_small_or_imprecise_dtypes=True)

            g.memset(ones_b[:, :], 1.0).then_inc(masks, 1)
            count(slot1[:, :], [[1, SLOTS]], 1).then_inc(masks, 1)
            count(spikes[:, :, H], [[0, TILES]], step=1).then_inc(masks, 1)
            count(spikes[:, :, H + 1], [[1, TILES]]).then_inc(masks, 1)
            count(token1[:, :], [[P, IDLE_TILES]], 1, 1).then_inc(masks, 1)
            g.memset(carry[:, :], 1.0).then_inc(masks, 1)
            g.memset(before[:, 0:1], 0.0).then_inc(masks, 1)
            count(place[:, :], [[1, EVENTS]]).then_inc(masks, 1)
            count(eight[:, :], [[1, JM]]).then_inc(masks, 1)
            count(part[:, :], [[0, 1]], step=1).then_inc(masks, 1)
            count(slot_no[:, :], [[P, ST]], step=1).then_inc(masks, 1)
            count(row_base[:, :], [[H, E]], -1).then_inc(masks, 1)
            count(desc[:, :], [[-1, E]], E).then_inc(masks, 1)
            g.memset(first_two[:, :], 0.0).then_inc(consts, 1)
            g.memset(faults[:, XG:XG + 1], 0.0).then_inc(masks, 1)
            g.memset(pair_info[:, :, 5, :], 1.0).then_inc(masks, 1)
            pool.wait_ge(consts, 10)
            g.memset(first_two[:, 0:1], 1.0).then_inc(masks, 1)
            g.memset(first_two[:, E + 1:E + 2], 1.0).then_inc(masks, 1)
            half = E // 2
            for i in range(2):
                g.memset(w1_got[:, i * half:(i + 1) * half, :], 0.0).then_inc(cleared, 1)
            pool.wait_ge(cleared, 2)
            for n, (e0, ne) in enumerate(GROUPS):
                pool.wait_ge(indexed, n + 1)
                for e in range(e0, e0 + ne):
                    g.indirect_dma_start(
                        out=w1_got[:, e, :], out_offset=None, in_=w1_rows[:, :],
                        in_offset=bass.IndirectOffsetOnAxis(ap=w1_index[:, e:e + 1], axis=0),
                        bounds_check=E * H - 1, oob_is_err=False, compute_op=ALU.bypass).then_inc(w1_in[e], 16)
            pool.wait_ge(copied, 16)
            pool.wait_ge(paired, 1)
            for e in range(E):
                pool.wait_ge(y_set, e + 1)
                if e:
                    pool.wait_ge(added, 16 * e)
                g.indirect_dma_start(
                    out=out_rows[:, :], out_offset=bass.IndirectOffsetOnAxis(ap=out_index[:, e:e + 1], axis=0),
                    in_=y[:, e % 3, :], in_offset=None, compute_op=ALU.add).then_inc(added, 16)
            pool.wait_ge(added, 16 * E)
        MASKS = 23

        @block.tensor
        def _(pe):
            pe.wait_ge(theta_set, 1)
            for g in range(XG):
                if g >= 3:
                    pe.wait_ge(theta_out, g - 2)
                for i in range(2):
                    j = 2 * g + i
                    mm = nc.tensor.matmul(DIF[g % 3][:, i * H:(i + 1) * H],
                                          spread[:, BPT * j:BPT * (j + 1), :].rearrange("k b t -> k (b t)"),
                                          theta3[:, :], start=True, stop=True)
                mm.then_inc(thetas, 1)

            def cumulate(g):
                pe.wait_ge(rates, g + 1)
                if g >= 3:
                    pe.wait_ge(checked, g - 2)
                nc.tensor.matmul(CUM[g % 3][:, 0:GW], cum_seq[:, :],
                                 rate[:, g % RING, :, :].rearrange("p j c -> p (j c)"),
                                 start=True, stop=True).then_inc(cums, 1)

            def difference(g):
                pe.wait_ge(floored, g + 1)
                if g < 3:
                    pe.wait_ge(theta_out, XG - (XG - 1 - g) % 3)
                else:
                    pe.wait_ge(spikes_out, g - 2)
                nc.tensor.matmul(DIF[g % 3][:, 0:GW], step_seq[:, :],
                                 floors[:, g % RING, :, :].rearrange("p j c -> p (j c)"),
                                 start=True, stop=True).then_inc(diffs, 1)

            pe.wait_ge(masks, 6)
            for g in range(XG):
                cumulate(g)
                if g:
                    difference(g - 1)
            pe.wait_ge(small_in, 64)
            for k in range(KC):
                mm = nc.tensor.transpose(bank[7][:, k * E:(k + 1) * E], router_rows[:, k * P:(k + 1) * P], ident[0:E, 0:E])
            mm.then_inc(router_t, 1)
            difference(XG - 1)
            pe.wait_ge(summed, XG)
            nc.tensor.matmul(count_ps, step_seq[:, :], floor_sum[:, :], start=True, stop=True).then_inc(counts, 1)
            pe.wait_ge(act_set, 1)
            pe.wait_ge(router_out, 1)
            pe.wait_ge(masks, MASKS)
            nc.tensor.matmul(within_ps, cum_tile[:, :], active[:, :], start=True, stop=True)
            nc.tensor.matmul(total_ps_s, ones_b[:, :], active[:, :], start=True, stop=True).then_inc(prefixed, 1)
            pe.wait_ge(spikes_out, XG)
            pe.wait_ge(info_set, 1)
            for j in range(TILES):
                pe.wait_ge(slotted, j + 1)
                for k in range(KC):
                    mm = nc.tensor.matmul(slotsT_ps[k], spikes[:, j, k * P:(k + 1) * P], to_slot[:, j, :],
                                          start=(j == 0), stop=(j == TILES - 1))
            mm.then_inc(compactT, 1)

            def compact_tile(j):
                for t in range(ST):
                    mm = nc.tensor.matmul(slots_ps[t], to_slot[:, j, t * P:(t + 1) * P], spikes[:, j, 0:H + 3],
                                          start=(j == 0), stop=(j == TILES - 1))
                return mm

            for j in range(TILES // 4):
                compact_tile(j)
            pe.wait_ge(spikesT_out, KC)
            pe.wait_ge(router_out, 1)
            for t in range(ST):
                for k in range(KC):
                    mm = nc.tensor.matmul(logit_s[:, t, :], spikesT[:, k, t * P:(t + 1) * P], routerT[:, k, :],
                                          start=(k == 0), stop=(k == KC - 1))
            mm.then_inc(logits, 1)
            for j in range(TILES // 4, TILES):
                mm = compact_tile(j)
            mm.then_inc(compact, 1)
            pe.wait_ge(idle_set, 1)
            for j in range(IDLE_TILES):
                mm = nc.tensor.matmul(idle_ps, to_idle[:, j, :], spikes[:, j, H:H + 2],
                                      start=(j == 0), stop=(j == IDLE_TILES - 1))
            mm.then_inc(idled, 1)

            def count_slots(dst, src):
                for t in range(ST):
                    mm = nc.tensor.matmul(dst[:, t, :], cum_tile[:, :], src[:, t, :], start=True, stop=(t == 0))
                    for before_t in range(t):
                        mm = nc.tensor.matmul(dst[:, t, :], ones_b[:, :], src[:, before_t, :],
                                              start=False, stop=(before_t == t - 1))
                return mm

            pe.wait_ge(chose, TOP_K)
            count_slots(rank_ps_s, chosen).then_inc(ranked, 1)
            pe.wait_ge(routes, 1)
            count_slots(place_ps, routed).then_inc(placed, 1)

            for n, (e0, ne) in enumerate(GROUPS):
                pe.wait_ge(maps_set, n + 1)
                if n >= 2:
                    pe.wait_ge(map_out, n - 1)
                to_map, to_info = maps_of(n)
                for e in range(e0, e0 + ne):
                    for dst, src in ((to_map[:, e - e0, :], to_pair[:, :, e, :]),
                                     (to_info[:, e - e0, 0:JM], chan_b[:, :, :]),
                                     (to_info[:, e - e0, JM:JM + 1], ev_start_b[:, :, e:e + 1])):
                        for i, edge in enumerate((from_start, from_end)):
                            for t in range(ST):
                                mm = nc.tensor.matmul(dst, edge[:, t, e, :], src[:, t, :],
                                                      start=(i == 0 and t == 0), stop=(i == 1 and t == ST - 1))
                mm.then_inc(mapped, 1)
            pe.wait_ge(info_set2, 1)
            for e in range(E):
                for t in range(ST):
                    mm = nc.tensor.matmul(pair_ps[:, e, :], to_pair[:, t, e, :], pair_info[:, t, :, e],
                                          start=(t == 0), stop=(t == ST - 1))
            mm.then_inc(pair_mm, 1)

            def hidden(e):
                pe.wait_ge(w1_in[e], 16)
                n = [n for n, (e0, ne) in enumerate(GROUPS) if e0 <= e < e0 + ne][0]
                pe.wait_ge(map_out, n + 1)
                ev_pair = maps_of(n, ev_maps)[0][:, e - GROUPS[n][0], :]
                for half in range(2):
                    if e >= 2:
                        pe.wait_ge(h_done, 2 * (e - 2) + half + 1)
                    for i in range(CH):
                        f = half * CH + i
                        mm = nc.tensor.matmul(HID[e % 2][half][:, i * PAIRS:(i + 1) * PAIRS],
                                              w1_got[:, e, f * P:(f + 1) * P], ev_pair, start=True, stop=True)
                    mm.then_inc(h_ready, 1)

            def project(e):
                pe.wait_ge(w2_in[e], 16)
                if e >= 2:
                    pe.wait_ge(yT_out, e - 1)
                if e == 1:
                    pe.wait_ge(verdict_set, 1)
                for k in range(KC):
                    for f in range(FC):
                        if k == 0 and f % CH == 0:
                            pe.wait_ge(h_done, 2 * e + f // CH + 1)
                        mm = nc.tensor.matmul(YT[e % 2][:, k * PAIRS:(k + 1) * PAIRS], w2_sb[:, e, f, k * P:(k + 1) * P],
                                              hT[:, e % 2, f, :], start=(f == 0), stop=(f == FC - 1))
                mm.then_inc(yT_ready, 1)

            def turn(e):
                pe.wait_ge(yT_out, e + 1)
                if e >= 2:
                    pe.wait_ge(y_set, e - 1)
                for k in range(KC):
                    mm = nc.tensor.transpose(YR[e % 2][:, k * P:(k + 1) * P], yT[:, e % 2, k, :], ident[:, :])
                mm.then_inc(y_turned, 1)

            hidden(0)
            pe.wait_ge(summed_up, 1)
            nc.tensor.matmul(verdict_ps, fine_sum[:, :], carry_f[:, :], start=True, stop=True).then_inc(verdict_mm, 1)
            for e in range(E):
                if e + 1 < E:
                    hidden(e + 1)
                if e:
                    turn(e - 1)
                project(e)
            turn(E - 1)

            pe.wait_ge(added, 16 * E)
            pe.wait_ge(verdict_set, 1)
            with pe.If(pe.value_load(verdict[0:1, 0:1]) != P * NV):
                pe.sem_inc(y_mm, 1)
                for k in range(KC):
                    mm = nc.tensor.transpose(bank[0][:, k * B:(k + 1) * B], cond3[0:B, k * P:(k + 1) * P], ident[0:B, 0:B])
                mm.then_inc(turned, 1)
                pe.wait_ge(turned_out, 1)
                with pe.Fori(0, TILES) as j:
                    pe.wait_ge(g_rates, j + 2)
                    for k in range(KC):
                        mm = nc.tensor.matmul(csum[:, k, :], g_rate[:, k * P:(k + 1) * P], cum_seq[:, :], start=True, stop=True)
                    mm.then_inc(g_cums, 1)
                    pe.wait_ge(g_xts, j + 1)
                    for k in range(KC):
                        mm = nc.tensor.matmul(logit, g_xt[:, k, :], routerT[:, k, :], start=(k == 0), stop=(k == KC - 1))
                    mm.then_inc(g_logits, 1)
                    pe.wait_ge(g_hot, j + 1)
                    nc.tensor.matmul(rank_ps, cum_tile[:, :], g_oh[:, :], start=True, stop=True)
                    nc.tensor.matmul(total_ps, ones_b[:, :], g_oh[:, :], start=True, stop=True).then_inc(g_ranks, 1)
                pe.wait_ge(g_routed, 1)
                with pe.Fori(0, E // 2) as pair:
                    for side in range(2):
                        with pe.Fori(0, NQ) as q:
                            step = (pair * 2 + side) * NQ + q
                            pe.wait_ge(w_in[side], pair * 32 + 32)
                            for f in range(FC):
                                if f < 2:
                                    pe.wait_ge(h_act, step * FC + 1)
                                else:
                                    pe.wait_ge(h_act, step * FC + f)
                                for k in range(KC):
                                    mm = nc.tensor.matmul(bank[f % 2][:, 0:GQ * P], g_w1[:, side, k, f * P:(f + 1) * P],
                                                          g_XT[:, k, bass.ds(q * (GQ * P), GQ * P)],
                                                          start=(k == 0), stop=(k == KC - 1))
                                mm.then_inc(h_mm, 1)
                            pe.wait_ge(h_act, step * FC + FC + 1)
                            pe.wait_ge(y_add, step * GQ + 1)
                            for s in range(GQ):
                                for f in range(FC):
                                    mm = nc.tensor.matmul(bank[2 + s][:, 0:H], g_h[:, f, s * P:(s + 1) * P], g_w2[:, side, f, :],
                                                          start=(f == 0), stop=(f == FC - 1))
                            mm.then_inc(y_mm, 1)

        @block.scalar
        def _(act):
            for i in range(3):
                act.dma_start(cond3[i * B:(i + 1) * B, :], cond).then_inc(small_in, 16)
            act.dma_start(router_rows[:, :], router_w).then_inc(small_in, 16)
            for g in range(XG):
                act.wait_ge(thetas, g + 1)
                nc.scalar.copy(theta_tok[:, 2 * g:2 * g + 2, :].rearrange("p j c -> p (j c)"), DIF[g % 3][:, 0:GW]).then_inc(theta_out, 1)

            def take_spikes(g):
                act.wait_ge(diffs, g + 1)
                nc.scalar.copy(spikes[:, 2 * g:2 * g + 2, 0:H], DIF[g % 3][:, 0:GW].rearrange("p (j c) -> p j c", j=2)).then_inc(spikes_out, 1)

            act.wait_ge(bias_set, 2)
            for g in range(XG):
                act.wait_ge(floored, g + 1)
                if g:
                    act.wait_ge(checked, g)
                nc.scalar.activation(over[:, :], CUM[g % 3][:, 0:GW], ACT.Relu, bias=run_max[:, :],
                                     accum_out=faults[:, g:g + 1]).then_inc(checked, 1)
                if g:
                    take_spikes(g - 1)
            take_spikes(XG - 1)
            nc.scalar.activation(warm[:, 1:2], warm[:, 0:1], ACT.Exp).then_inc(warmed, 1)
            for k in range(KC):
                act.wait_ge(compactT, 1)
                nc.scalar.activation(spikesT[:, k, :], slotsT_ps[k], ACT.Copy, scale=SPIKE).then_inc(spikesT_out, 1)
            act.wait_ge(shift_set, 1)
            nc.scalar.activation(expo[:, :, :], shifted[:, :, :], ACT.Exp).then_inc(exps, 1)
            act.wait_ge(warmed, 1)
            nc.scalar.activation(warm[:, 2:3], warm[:, 0:1], ACT.Gelu).then_inc(warmed, 1)
            for n, (e0, ne) in enumerate(GROUPS):
                act.wait_ge(mapped, n + 1)
                nc.scalar.copy(ev_maps[n][:, :], MAP[n][:, 0:ne * (PAIRS + JM + 1)]).then_inc(map_out, 1)
            for e in range(E):
                if e >= 2:
                    act.wait_ge(yT_ready, e - 1)
                for half in range(2):
                    act.wait_ge(h_ready, 2 * e + half + 1)
                    nc.scalar.activation(hT[:, e % 2, half * CH:(half + 1) * CH, :].rearrange("p f n -> p (f n)"),
                                         HID[e % 2][half][:, 0:CH * PAIRS], ACT.Gelu, scale=SPIKE).then_inc(h_done, 1)

            act.wait_ge(added, 16 * E)
            act.wait_ge(verdict_set, 1)
            with act.If(act.value_load(verdict[0:1, 0:1]) != P * NV):
                act.sem_inc(h_act, 1)
                with act.Fori(0, TILES) as j:
                    act.wait_ge(g_max, j + 1)
                    nc.scalar.activation(g_e[:, :], logit, ACT.Exp, bias=g_one[:, 1:2]).then_inc(g_exps, 1)
                with act.Fori(0, E * NQ) as step:
                    for f in range(FC):
                        act.wait_ge(h_mm, step * FC + f + 1)
                        if f == 0:
                            act.wait_ge(y_mm, step + 1)
                        nc.scalar.activation(g_h[:, f, :], bank[f % 2][:, 0:GQ * P], ACT.Gelu).then_inc(h_act, 1)

        @block.vector
        def _(dve):
            v = nc.vector
            steps = [0]

            def link(ins):
                steps[0] += 1
                ins.then_inc(vec, 1)
                dve.wait_ge(vec, steps[0])

            def loose(ins):
                steps[0] += 1
                ins.then_inc(vec, 1)

            v.memset(run_max[:, :], -RUN_MAX).then_inc(bias_set, 1)
            v.memset(warm[:, 0:1], 0.0).then_inc(bias_set, 1)
            loose(v.memset(carry_f[:, :], 1.0))
            dve.wait_ge(masks, 3)
            loose(v.tensor_copy(spread[:, :, :], ident3[:, :].unsqueeze(2).to_broadcast([3 * B, B, T])))
            dve.wait_ge(small_in, 64)
            link(v.tensor_scalar(theta[:, :], cond3[:, :], -1.0, 1.0, ALU.mult, ALU.add))
            link(v.tensor_scalar(theta[:, :], theta[:, :], -HALF_ULP, None, ALU.add))
            link(v.tensor_copy(theta_hi[:, :], theta[:, :]))
            link(v.tensor_tensor(theta_r[:, :], theta[:, :], theta_hi[:, :], ALU.subtract))
            link(v.tensor_copy(theta_mid[:, :], theta_r[:, :]))
            loose(v.tensor_copy(theta3[0:B, :], theta_hi[0:B, :]))
            loose(v.tensor_copy(theta3[B:2 * B, :], theta_mid[B:2 * B, :]))
            v.tensor_tensor(theta3[2 * B:, :], theta_r[2 * B:, :], theta_mid[2 * B:, :], ALU.subtract).then_inc(theta_set, 1)

            def take_rates(g):
                dve.wait_ge(x_in[g // 2], 16)
                v.tensor_scalar(rate[:, g % RING, :, :], x_sb[:, 2 * g:2 * g + 2, :], 0.0, float(DT),
                                ALU.max, ALU.mult).then_inc(rates, 1)

            take_rates(0)
            take_rates(1)
            for g in range(XG):
                dve.wait_ge(cums, g + 1)
                dve.wait_ge(theta_out, g + 1)
                if g >= RING:
                    dve.wait_ge(diffs, g - RING + 1)
                v.tensor_tensor(floors[:, g % RING, :, :].rearrange("p j c -> p (j c)"), CUM[g % 3][:, 0:GW],
                                theta_tok[:, 2 * g:2 * g + 2, :].rearrange("p j c -> p (j c)"), ALU.is_ge).then_inc(floored, 1)
                if g + 2 < XG:
                    take_rates(g + 2)
                dve.wait_ge(floored, g + 1)
                with nc.allow_low_precision(reason="counts up to 256 are exact in bfloat16"):
                    v.tensor_reduce(floor_sum[:, 2 * g:2 * g + 2], floors[:, g % RING, :, :], AX_X, ALU.add).then_inc(summed, 1)

            dve.wait_ge(router_t, 1)
            v.tensor_copy(routerT[:, :, :], bank[7][:, 0:KC * E].rearrange("p (k e) -> p k e", k=KC)).then_inc(router_out, 1)
            dve.wait_ge(counts, 1)
            v.tensor_scalar(active[:, :], count_ps, 0.5, None, ALU.is_gt).then_inc(act_set, 1)
            v.tensor_copy(spikes[:, :, H + 2], count_ps).then_inc(info_set, 1)
            dve.wait_ge(act_set, 1)
            dve.wait_ge(masks, MASKS)
            dve.wait_ge(prefixed, 1)
            link(v.tensor_tensor_scan(before[:, 1:TILES + 1], carry[:, :], total_ps_s, 0.0, ALU.mult, ALU.add))
            link(v.tensor_tensor(rank_t[:, :], within_ps, before[:, 0:TILES], ALU.add))
            link(v.tensor_tensor(slot_of[:, :], rank_t[:, :], active[:, :], ALU.mult))
            for j in range(TILES):
                v.tensor_scalar(to_slot[:, j, :], slot1[:, :], slot_of[:, j:j + 1], None, ALU.is_equal).then_inc(slotted, 1)
            loose(v.tensor_tensor(idle_a[:, :], token1[:, :], rank_t[:, 0:IDLE_TILES], ALU.subtract))
            link(v.tensor_scalar(idle_b[:, :], active[:, 0:IDLE_TILES], -1.0, 1.0, ALU.mult, ALU.add))
            link(v.tensor_tensor(idle_rank[:, :], idle_a[:, :], idle_b[:, :], ALU.mult))
            for j in range(IDLE_TILES):
                ins = v.tensor_scalar(to_idle[:, j, :], slot1[:, 0:PAIRS], idle_rank[:, j:j + 1], None, ALU.is_equal)
            ins.then_inc(idle_set, 1)
            loose(v.tensor_scalar(unused[:, :], slot_no[:, :], before[:, TILES:TILES + 1], FAR, ALU.is_ge, ALU.mult))

            C = XG
            link(v.tensor_scalar(in_range[:, :], cond3[:, :], 0.0, None, ALU.is_ge))
            link(v.scalar_tensor_tensor(theta_r[:, :], cond3[:, :], 1.0, in_range[:, :], ALU.is_lt, ALU.mult))
            link(v.tensor_reduce(theta[:, 0:1], theta_r[:, :], AX_X, ALU.add))
            loose(v.tensor_scalar(faults[0:3 * B, C:C + 1], theta[:, 0:1], -1.0, float(H), ALU.mult, ALU.add))
            C += 1
            loose(v.tensor_scalar(faults[:, C:C + 1], before[:, TILES:TILES + 1], -float(SLOTS), None, ALU.add))
            C += 1

            dve.wait_ge(logits, 1)
            link(v.tensor_reduce(top_l[:, :], logit_s, AX_X, ALU.max))
            v.tensor_tensor(shifted[:, :, :], logit_s, top_l[:, :].unsqueeze(2).to_broadcast([P, ST, E]),
                            ALU.subtract).then_inc(shift_set, 1)
            dve.wait_ge(exps, 1)
            for t in range(ST):
                loose(v.max(best[:, t, :], expo[:, t, :]))
            dve.wait_ge(vec, steps[0])
            for t in range(ST):
                loose(v.max_index(best_at[:, t, :], best[:, t, :], expo[:, t, :]))
            dve.wait_ge(vec, steps[0])
            link(v.tensor_copy(best_f[:, :, :], best_at[:, :, 0:TOP_K]))
            for k in range(TOP_K):
                v.tensor_tensor(chosen[:, :, k * E:(k + 1) * E], eight[:, :].unsqueeze(1).to_broadcast([P, ST, E]),
                                best_f[:, :, k].unsqueeze(2).to_broadcast([P, ST, E]), ALU.is_equal).then_inc(chose, 1)

            dve.wait_ge(compact, 1)
            for t in range(ST):
                loose(v.tensor_copy(slot_info[:, t, :], slots_ps[t][:, H:H + 3]))
            dve.wait_ge(vec, steps[0])
            link(v.scalar_tensor_tensor(token_no[:, :], slot_info[:, :, 1], float(P), slot_info[:, :, 0], ALU.mult, ALU.add))
            link(v.tensor_tensor(inactive[:, :], token_no[:, :], slot_no[:, :], ALU.subtract))
            for t in range(ST):
                loose(v.tensor_scalar(base[:, t, :], first_two[:, :], inactive[:, t:t + 1], unused[:, t:t + 1], ALU.mult, ALU.add))
            dve.wait_ge(vec, steps[0])
            dve.wait_ge(chose, TOP_K)
            dve.wait_ge(ranked, 1)
            link(v.tensor_tensor(rank_s[:, :, :], rank_ps_s, base[:, :, :], ALU.add))
            link(v.scalar_tensor_tensor(kept[:, :, :], rank_s[:, :, :], float(CAP), chosen[:, :, :], ALU.is_le, ALU.mult))
            link(v.tensor_tensor(routed[:, :, 0:E], kept[:, :, 0:E], kept[:, :, E:2 * E], ALU.add))
            v.tensor_tensor(routed[:, :, E:2 * E], routed[:, :, 0:E],
                            slot_info[:, :, 2].unsqueeze(2).to_broadcast([P, ST, E]), ALU.mult).then_inc(routes, 1)
            for t in range(ST):
                loose(v.tensor_tensor(keyed[:, t, :], slots_ps[t][:, 0:H], slot1[:, 0:H], ALU.mult))
            dve.wait_ge(vec, steps[0])
            for t in range(ST):
                loose(v.max(chan[:, t, :], keyed[:, t, :]))
            dve.wait_ge(vec, steps[0])
            link(v.tensor_copy(chan_b[:, :, :], chan[:, :, :]))

            dve.wait_ge(routes, 1)
            dve.wait_ge(placed, 1)
            link(v.tensor_copy(places[:, :, :], place_ps))
            loose(v.tensor_tensor(pair_at[:, :, :], places[:, :, 0:E], routed[:, :, 0:E], ALU.mult))
            link(v.tensor_tensor(ev_start[:, :, :], places[:, :, E:2 * E], routed[:, :, E:2 * E], ALU.subtract))
            link(v.tensor_copy(ev_start_b[:, :, :], ev_start[:, :, :]))

            def make_maps(n):
                e0, ne = GROUPS[n]
                for e in range(e0, e0 + ne):
                    for t in range(ST):
                        v.tensor_scalar(from_start[:, t, e, :], place[:, :], ev_start[:, t, e:e + 1], None, ALU.is_ge)
                        v.tensor_scalar(from_end[:, t, e, :], place[:, :], places[:, t, E + e:E + e + 1], -1.0, ALU.is_ge, ALU.mult)
                        ins = v.tensor_scalar(to_pair[:, t, e, :], slot1[:, 0:PAIRS], pair_at[:, t, e:e + 1], None, ALU.is_equal)
                ins.then_inc(maps_set, 1)

            def make_indices(n):
                e0, ne = GROUPS[n]
                es = slice(e0, e0 + ne)
                _, info = maps_of(n, ev_maps)
                dve.wait_ge(map_out, n + 1)
                link(v.tensor_scalar(nth[:, es], info[:, :, JM], -1.0, part[:, 0:1], ALU.mult, ALU.add))
                link(v.tensor_tensor(nth_hit[:, es, :], eight[:, :].unsqueeze(1).to_broadcast([P, ne, JM]),
                                     nth[:, es].unsqueeze(2).to_broadcast([P, ne, JM]), ALU.is_equal))
                link(v.tensor_tensor(nth_chan[:, es, :], info[:, :, 0:JM], nth_hit[:, es, :], ALU.mult))
                link(v.tensor_reduce(ev_chan[:, es], nth_chan[:, es, :], AX_X, ALU.add))
                loose(v.tensor_scalar(ev_far[:, es], ev_chan[:, es], 0.0, FAR, ALU.is_equal, ALU.mult))
                link(v.tensor_tensor(ev_row[:, es], ev_chan[:, es], row_base[:, es], ALU.add))
                v.tensor_tensor(w1_index[:, es], ev_row[:, es], ev_far[:, es], ALU.add).then_inc(indexed, 1)

            make_maps(0)
            link(v.tensor_tensor(top_sum[:, :], best[:, :, 0], best[:, :, 1], ALU.add))
            link(v.reciprocal(top_inv[:, :], top_sum[:, :]))
            make_indices(0)
            make_maps(1)
            loose(v.tensor_tensor(gate1[:, :], best[:, :, 0], top_inv[:, :], ALU.mult))
            link(v.tensor_tensor(gate2[:, :], best[:, :, 1], top_inv[:, :], ALU.mult))
            make_indices(1)
            make_maps(2)
            for k, (dst, gate) in enumerate(((gates_a, gate1), (gates_b, gate2))):
                loose(v.tensor_tensor(dst[:, :, :], kept[:, :, k * E:(k + 1) * E],
                                      gate[:, :].unsqueeze(2).to_broadcast([P, ST, E]), ALU.mult))
            make_indices(2)
            dve.wait_ge(vec, steps[0])
            link(v.tensor_tensor(gates[:, :, :], gates_a[:, :, :], gates_b[:, :, :], ALU.add))
            link(v.tensor_copy(pair_info[:, :, 0, :], gates[:, :, :]))
            link(v.tensor_tensor(gates_r[:, :, :], gates[:, :, :], pair_info[:, :, 0, :], ALU.subtract))
            link(v.tensor_copy(pair_info[:, :, 1, :], gates_r[:, :, :]))
            loose(v.tensor_tensor(pair_info[:, :, 2, :], gates_r[:, :, :], pair_info[:, :, 1, :], ALU.subtract))
            dve.wait_ge(idled, 1)
            link(v.tensor_copy(idle_in[:, :], idle_ps))
            for i in range(2):
                ins = v.tensor_copy(pair_info[:, :, 3 + i, :], slot_info[:, :, i].unsqueeze(2).to_broadcast([P, ST, E]))
                if i == 0:
                    loose(ins)
            ins.then_inc(info_set2, 1)

            link(v.tensor_scalar(chan_hit[:, :, :], chan[:, :, :], 0.0, None, ALU.is_gt))
            link(v.tensor_reduce(hits[:, :], chan_hit[:, :, :], AX_X, ALU.add))
            loose(v.tensor_tensor(faults[:, C:C + ST], hits[:, :], slot_info[:, :, 2], ALU.not_equal))
            C += ST
            for ends, room in ((0, PAIRS), (E, EVENTS)):
                loose(v.tensor_scalar(faults[:, C:C + ST * E].rearrange("p (t e) -> p t e", t=ST),
                                      places[:, :, ends:ends + E], -float(room), None, ALU.add))
                C += ST * E
            assert C == NV
            dve.wait_ge(vec, steps[0])
            dve.wait_ge(checked, XG)
            link(v.tensor_scalar(fine[:, :], faults[:, :], 0.0, None, ALU.is_le))
            v.tensor_reduce(fine_sum[:, :], fine[:, :], AX_X, ALU.add).then_inc(summed_up, 1)

            link(v.scalar_tensor_tensor(idle_row[:, :], idle_in[:, 1:2], float(P), idle_in[:, 0:1], ALU.mult, ALU.add))
            dve.wait_ge(pair_mm, 1)
            link(v.tensor_copy(pairs[:, :, :], pair_ps))
            loose(v.tensor_scalar(pair_free[:, :], pairs[:, :, 5], -1.0, 1.0, ALU.mult, ALU.add))
            loose(v.scalar_tensor_tensor(pair_row[:, :], pairs[:, :, 4], float(P), pairs[:, :, 3], ALU.mult, ALU.add))
            link(v.tensor_tensor(pair_a[:, :], pairs[:, :, 0], pairs[:, :, 1], ALU.add))
            loose(v.tensor_tensor(pair_gate[:, :], pair_a[:, :], pairs[:, :, 2], ALU.add))
            v.scalar_tensor_tensor(out_index[:, :], pair_free[:, :], idle_row[:, 0:1], pair_row[:, :],
                                   ALU.mult, ALU.add).then_inc(paired, 1)
            dve.wait_ge(vec, steps[0])

            def take_yT(e):
                dve.wait_ge(yT_ready, e + 1)
                if e >= 2:
                    dve.wait_ge(y_turned, e - 1)
                v.tensor_copy(yT[:, e % 2, :, :].rearrange("p k n -> p (k n)"), YT[e % 2][:, 0:KC * PAIRS]).then_inc(yT_out, 1)

            def take_y(e):
                dve.wait_ge(y_turned, e + 1)
                if e >= 3:
                    dve.wait_ge(added, 16 * (e - 2))
                v.tensor_scalar(y[:, e % 3, :], YR[e % 2], pair_gate[:, e:e + 1], None,
                                ALU.mult).then_inc(y_set, 1)

            dve.wait_ge(verdict_mm, 1)
            link(v.tensor_copy(fine_all[:, :], verdict_ps))
            v.tensor_copy(verdict[:, :], fine_all[:, :]).then_inc(verdict_set, 1)
            for e in range(E):
                take_yT(e)
                take_y(e)

            dve.wait_ge(added, 16 * E)
            dve.wait_ge(verdict_set, 1)
            with dve.If(dve.value_load(verdict[0:1, 0:1]) != P * NV):
                dve.sem_inc(g_rates, 1)
                dve.sem_inc(y_add, 1)
                dve.wait_ge(turned, 1)
                setup = [0]

                def set_up(ins):
                    setup[0] += 1
                    ins.then_inc(turned_out, 1)
                    dve.wait_ge(turned_out, setup[0])

                set_up(v.tensor_copy(stateT[:, :, :], bank[0][:, 0:KC * B].rearrange("p (k b) -> p k b", k=KC)))
                set_up(v.tensor_copy(gs_i[:, :, :], stateT[:, :, :]))
                set_up(v.tensor_copy(gs_f[:, :, :], gs_i[:, :, :]))
                set_up(v.tensor_tensor(gs_gt[:, :, :], gs_f[:, :, :], stateT[:, :, :], ALU.is_gt))
                set_up(v.tensor_tensor(floor_stateT[:, :, :], gs_f[:, :, :], gs_gt[:, :, :], ALU.subtract))
                set_up(v.memset(g_seen[:, :], 0.0))
                with dve.Fori(0, TILES) as j:
                    done = [0]

                    def link(ins):
                        done[0] += 1
                        ins.then_inc(g_vec, 1)
                        dve.wait_ge(g_vec, j * V + done[0])

                    one = lambda n: g_one[:, n:n + 1]
                    dve.wait_ge(gx_in, j * 16 + 16)
                    v.tensor_scalar(g_rate[:, :], g_x[:, :], 0.0, float(DT), ALU.max, ALU.mult).then_inc(g_rates, 1)
                    dve.wait_ge(g_cums, j + 1)
                    for k in range(KC):
                        link(v.tensor_tensor(
                            g_c[:, k, :].rearrange("p (b t) -> p b t", b=BPT), csum[:, k, :].rearrange("p (b t) -> p b t", b=BPT),
                            stateT[:, k, bass.ds(j * BPT, BPT)].unsqueeze(2).to_broadcast([P, BPT, T]), ALU.add))
                    link(v.tensor_copy(g_ci[:, :, :], g_c[:, :, :]))
                    link(v.tensor_copy(g_cf[:, :, :], g_ci[:, :, :]))
                    link(v.tensor_tensor(g_gt[:, :, :], g_cf[:, :, :], g_c[:, :, :], ALU.is_gt))
                    link(v.tensor_tensor(g_fl[:, :, :], g_cf[:, :, :], g_gt[:, :, :], ALU.subtract))
                    fl = g_fl[:, :, :].rearrange("p k (b t) -> p (k b) t", b=BPT)
                    spk = g_sp[:, :, :].rearrange("p k (b t) -> p (k b) t", b=BPT)
                    link(v.tensor_tensor(spk[:, :, 1:T], fl[:, :, 1:T], fl[:, :, 0:T - 1], ALU.subtract))
                    for k in range(KC):
                        link(v.tensor_tensor(spk[:, k * BPT:(k + 1) * BPT, 0], fl[:, k * BPT:(k + 1) * BPT, 0],
                                                     floor_stateT[:, k, bass.ds(j * BPT, BPT)], ALU.subtract))
                    v.tensor_scalar(g_xt[:, :, :], g_sp[:, :, :], SPIKE, None, ALU.mult).then_inc(g_xts, 1)
                    dve.wait_ge(g_xts, j + 1)
                    link(v.tensor_copy(g_XT[:, :, bass.ds(j * P, P)], g_xt[:, :, :]))
                    dve.wait_ge(g_logits, j + 1)
                    link(v.tensor_reduce(one(0), logit, AX_X, ALU.max))
                    v.tensor_scalar(one(1), one(0), -1.0, None, ALU.mult).then_inc(g_max, 1)
                    dve.wait_ge(g_exps, j + 1)
                    link(v.tensor_reduce(one(2), g_e[:, :], AX_X, ALU.max))
                    link(v.scalar_tensor_tensor(g_key[:, :], g_e[:, :], one(2), desc[:, :], ALU.is_equal, ALU.mult))
                    link(v.tensor_reduce(one(3), g_key[:, :], AX_X, ALU.max))
                    link(v.tensor_scalar(g_oh[:, 0:E], desc[:, :], one(3), None, ALU.is_equal))
                    link(v.scalar_tensor_tensor(g_e2[:, :], g_oh[:, 0:E], -2.0, g_e[:, :], ALU.mult, ALU.add))
                    link(v.tensor_reduce(one(4), g_e2[:, :], AX_X, ALU.max))
                    link(v.scalar_tensor_tensor(g_key[:, :], g_e2[:, :], one(4), desc[:, :], ALU.is_equal, ALU.mult))
                    link(v.tensor_reduce(one(5), g_key[:, :], AX_X, ALU.max))
                    v.tensor_scalar(g_oh[:, E:2 * E], desc[:, :], one(5), None, ALU.is_equal).then_inc(g_hot, 1)
                    link(v.tensor_tensor(one(6), one(2), one(4), ALU.add))
                    link(v.reciprocal(one(7), one(6)))
                    link(v.tensor_tensor(one(8), one(2), one(7), ALU.mult))
                    link(v.tensor_tensor(one(9), one(4), one(7), ALU.mult))
                    dve.wait_ge(g_ranks, j + 1)
                    dve.wait_ge(g_hot, j + 1)
                    link(v.tensor_tensor(g_rank[:, :], rank_ps, g_seen[:, :], ALU.add))
                    link(v.tensor_tensor(g_seen[:, :], total_ps, g_seen[:, :], ALU.add))
                    link(v.scalar_tensor_tensor(g_kept[:, :], g_rank[:, :], float(CAP), g_oh[:, :], ALU.is_le, ALU.mult))
                    link(v.tensor_scalar(g_tmp[:, :], g_kept[:, 0:E], one(8), None, ALU.mult))
                    link(v.scalar_tensor_tensor(g_gates[:, bass.ds(j * E, E)], g_kept[:, E:2 * E], one(9), g_tmp[:, :], ALU.mult, ALU.add))
                    assert done[0] == V, done
                v.tensor_copy(g_one[:, 10:11], g_one[:, 9:10]).then_inc(g_routed, 1)
                gates3 = g_gates[:, :].rearrange("p (j e) -> p j e", e=E)
                with dve.Fori(0, E) as e:
                    with dve.Fori(0, NQ) as q:
                        step = e * NQ + q
                        dve.wait_ge(y_add, step * GQ + 1)
                        v.tensor_copy(g_gcol[:, :], gates3[:, bass.ds(q * GQ, GQ), bass.ds(e, 1)].rearrange("p a b -> p (a b)")).then_inc(g_routed, 1)
                        dve.wait_ge(g_routed, step + 2)
                        dve.wait_ge(y_mm, step + 2)
                        for s in range(GQ):
                            a = g_acc[:, bass.ds(q * GQ + s, 1), :].rearrange("p a c -> p (a c)")
                            v.scalar_tensor_tensor(a, bank[2 + s][:, 0:H], g_gcol[:, s:s + 1], a, ALU.mult, ALU.add).then_inc(y_add, 1)



_INS = ["x", "cond_1024", "L0_ffn_router_w", "L0_ffn_w1", "L0_ffn_w2"]
_OUTS = [((32, 64, 256), "float32")]


def kernel(**inputs):
    import numpy as _np
    import concourse.bacc as _bacc
    from concourse import mybir as _mybir
    from concourse.bass_utils import run_bass_kernel_spmd as _run

    nc = _bacc.Bacc("TRN2", target_bir_lowering=False, num_devices=1)
    arrays, args = {}, []
    for name in _INS:
        a = _np.ascontiguousarray(inputs[name])
        arrays[f"in_{name}_dram"] = a
        args.append(nc.dram_tensor(f"in_{name}_dram", a.shape, _mybir.dt.from_np(a.dtype), kind="ExternalInput").ap())
    for i, (shape, dtype) in enumerate(_OUTS):
        dt = _mybir.dt.from_np(_np.dtype(dtype))
        args.append(nc.dram_tensor(f"out_{i}_dram", shape, dt, kind="ExternalOutput").ap())
    adaln_ffn_kernel(nc, *args)
    r = _run(nc, [arrays], core_ids=[0])
    return r.results[0]["out_0_dram"]
```

```python
from contextlib import ExitStack

import concourse.bass as bass
import numpy as np
from concourse import mybir

F32 = mybir.dt.float32
F32R = mybir.dt.float32r
BF16 = mybir.dt.bfloat16
I32 = mybir.dt.int32
U32 = mybir.dt.uint32
ALU = mybir.AluOpType
ACT = mybir.ActivationFunctionType
AX_X = mybir.AxisListType.X

P = 128
DT = np.float32(0.001)
SPIKE = float(np.float32(1.0) / DT)
TOP_K = 2
CAP_FACTOR = 1.25
HALF_ULP = 2.0 ** -25
RUN_MAX = 0.49
FAR = 4096.0


def adaln_ffn_kernel(nc, x, cond, router_w, w1, w2, out):
    B, T, H = x.shape
    E, _, FFN = w1.shape
    N = B * T
    TILES = N // P
    BPT = P // T
    KC = H // P
    FC = FFN // P
    CH = FC // 2
    CAP = max(1, int(CAP_FACTOR * N / E * TOP_K))
    ST = 2
    SLOTS = ST * P
    PAIRS = P
    EVENTS = P
    JM = 8
    D = E // 2
    INFO = PAIRS + JM + 2
    X_MAX = RUN_MAX / (T * float(DT)) - 0.05
    PARTS = ((0, 10), (10, TILES))
    WARM_START = 8
    WARM = (3, 3, 1)
    POOL_TILES = 1
    XG = TILES // 2
    GW = 2 * H

    x_tiles = x.rearrange("(j h) t c -> (h t) j c", h=BPT)
    out_tiles = out.rearrange("(j h) t c -> (h t) j c", h=BPT)
    out_rows = out.rearrange("b t c -> (b t) c")
    w1_rows = w1.rearrange("e h f -> (e h) f")

    with ExitStack() as ctx:
        def sb(name, shape, dt=F32):
            return ctx.enter_context(nc.sbuf_tensor(name, shape, dt))

        def psum(name, shape, dt=F32):
            return ctx.enter_context(nc.psum_tensor(name, shape, dt))

        def sem(name):
            return ctx.enter_context(nc.semaphore(name))

        cum_seq = sb("cum_seq", [P, P])
        cum_tile = sb("cum_tile", [P, P], BF16)
        step_seq = sb("step_seq", [P, P], BF16)
        ones_b = sb("ones_b", [P, P], BF16)
        zeros_b = sb("zeros_b", [P, 2 * E], BF16)
        ident = sb("ident", [P, P])
        ident3 = sb("ident3", [3 * B, B], BF16)
        slot1 = sb("slot1", [P, SLOTS], BF16)
        place = sb("place", [P, EVENTS], BF16)
        eight = sb("eight", [P, JM])
        part = sb("part", [P, 1])
        slot_no = sb("slot_no", [P, ST])
        key_diag = sb("key_diag", [P, KC, P], BF16)
        first_two = sb("first_two", [P, TOP_K * E])
        desc = sb("desc", [P, E])
        carry = sb("carry", [P, TILES])

        cond3 = sb("cond3", [3 * B, H])
        theta = sb("theta", [3 * B, H])
        theta_r = sb("theta_r", [3 * B, H])
        theta_mid = sb("theta_mid", [3 * B, H], BF16)
        theta3 = sb("theta3", [3 * B, H], BF16)
        in_range = sb("in_range", [3 * B, H])
        spread = sb("spread", [3 * B, B, T], BF16)
        router_rows = sb("router_rows", [E, H])
        routerT = sb("routerT", [P, KC, E])
        router_s = sb("router_s", [P, KC, E])
        router_r = sb("router_r", [P, KC, E])
        router3 = sb("router3", [P, 3, KC, E], BF16)
        x_sb = sb("x_sb", [P, TILES, H])
        RING = 4
        rate = sb("rate", [P, RING, 2, H])
        theta_tok = sb("theta_tok", [P, TILES, H])
        XW = H + 4
        floors = sb("floors", [P, RING, 2, H], BF16)
        spikes = sb("spikes", [P, TILES, XW], BF16)
        x_bound = sb("x_bound", [P, 1])
        count = sb("count", [P, TILES])
        active = sb("active", [P, TILES], BF16)
        before = sb("before", [P, TILES + 1])
        rank_t = sb("rank_t", [P, TILES])
        slot_of = sb("slot_of", [P, TILES])
        to_slot = sb("to_slot", [P, TILES, SLOTS], BF16)
        spikesT = sb("spikesT", [P, KC, SLOTS], BF16)
        slot_info = sb("slot_info", [P, ST, 3])
        chan = sb("chan", [P, ST, JM])
        chan_hit = sb("chan_hit", [P, ST, JM])
        hits = sb("hits", [P, ST])
        top_l = sb("top_l", [P, ST])
        shifted = sb("shifted", [P, ST, E])
        expo = sb("expo", [P, ST, E])
        best = sb("best", [P, ST, JM])
        best_at = sb("best_at", [P, ST, JM], U32)
        chosen = sb("chosen", [P, ST, TOP_K * E], BF16)
        token_no = sb("token_no", [P, ST])
        inactive = sb("inactive", [P, ST])
        unused = sb("unused", [P, ST])
        base = sb("base", [P, ST, TOP_K * E])
        rank_s = sb("rank_s", [P, ST, TOP_K * E])
        kept = sb("kept", [P, ST, TOP_K * E])
        routed = sb("routed", [P, ST, 2 * E], BF16)
        pair_at = sb("pair_at", [P, ST, E])
        places = sb("places", [P, ST, 2 * E])
        ev_start = sb("ev_start", [P, ST, E])
        top_sum = sb("top_sum", [P, ST])
        top_inv = sb("top_inv", [P, ST])
        gate1 = sb("gate1", [P, ST])
        gate2 = sb("gate2", [P, ST])
        gates_a = sb("gates_a", [P, ST, E])
        gates_b = sb("gates_b", [P, ST, E])
        gates = sb("gates", [P, ST, E])
        gates_r = sb("gates_r", [P, ST, E])
        PI = 4
        pair_info = sb("pair_info", [P, ST, PI, E], BF16)
        slot_map = sb("slot_map", [P, ST, E, INFO], BF16)
        from_start = sb("from_start", [P, ST, E, EVENTS], BF16)
        spare_theta = theta_tok[:, :, :].rearrange("p j c -> p (j c)")
        from_end = spare_theta[:, 2 * FC * PAIRS:2 * FC * PAIRS + ST * E * EVENTS // 2].bitcast(BF16).rearrange(
            "p (t e n) -> p t e n", t=ST, e=E)
        ev_pair = sb("ev_pair", [P, D, PAIRS])
        nth = sb("nth", [P, D])
        nth_chan = sb("nth_chan", [P, D, JM])
        ev_chan = sb("ev_chan", [P, D])
        ev_base = sb("ev_base", [P, D])
        w1_index = sb("w1_index", [P, D], I32)
        w1_got = sb("w1_got", [P, D, FFN])
        WR = 4
        w2_sb = sb("w2_sb", [P, WR, FC, H])
        w2_hi = sb("w2_hi", [P, 3, FC, H], F32R)
        w2_lo = sb("w2_lo", [P, 2, FC, H], F32R)
        hT_hi = sb("hT_hi", [P, 2, FC, PAIRS], F32R)
        hT_lo = sb("hT_lo", [P, 2, FC, PAIRS], F32R)
        hT = spare_theta[:, 0:2 * FC * PAIRS].rearrange(
            "p (d f n) -> p d f n", d=2, f=FC)
        y, y_even = rate[:, 0, :, :], rate[:, 1, :, :]
        y_hi = sb("y_hi", [PAIRS, 2, H], F32R)
        y_lo = sb("y_lo", [PAIRS, 2, H], F32R)
        pairs = sb("pairs", [PAIRS, E, PI])
        pair_a = sb("pair_a", [PAIRS, E])
        pair_gate = sb("pair_gate", [PAIRS, E])
        pair_slot = sb("pair_slot", [PAIRS, D])
        to_out = sb("to_out", [PAIRS, D, SLOTS], F32R)
        ffn_out = floors[:, 0:2, :, :].rearrange("p a b c -> p (a b c)").bitcast(F32).rearrange(
            "p (t c) -> p t c", t=ST)
        out_index = sb("out_index", [P, ST], I32)
        NV = 1 + 1 + ST + 1 + 2 * ST * E
        faults = sb("faults", [P, NV])
        fine = sb("fine", [P, NV])
        fine_sum = sb("fine_sum", [P, 1])
        fine_all = sb("fine_all", [1, 1])
        verdict = sb("verdict", [1, 1], I32)
        warm = sb("warm", [P, 3])
        carry_f = sb("carry_f", [P, 1])

        gs_i = sb("gs_i", [P, KC, B], I32)
        gs_f = sb("gs_f", [P, KC, B])
        gs_gt = sb("gs_gt", [P, KC, B])
        stateT = sb("stateT", [P, KC, B])
        floor_stateT = sb("floor_stateT", [P, KC, B])
        g_ci = sb("g_ci", [P, KC, P], I32)
        spare = rate[:, :, :, :].rearrange("p r a c -> p (r a) c")
        g_x, g_rate = spare[:, 0, :], spare[:, 1, :]
        g_c, g_cf, g_gt, g_fl, g_sp, g_xt = (spare[:, 2 + i, :].rearrange("p (k n) -> p k n", k=KC) for i in range(6))
        g_e = sb("g_e", [P, E])
        g_e2 = sb("g_e2", [P, E])
        g_key = sb("g_key", [P, E])
        g_one = sb("g_one", [P, 12])
        g_oh = sb("g_oh", [P, TOP_K * E], BF16)
        g_rank = sb("g_rank", [P, TOP_K * E])
        g_seen = sb("g_seen", [P, TOP_K * E])
        g_kept = sb("g_kept", [P, TOP_K * E])
        g_tmp = sb("g_tmp", [P, E])
        g_gates = sb("g_gates", [P, TILES * E])
        GQ = 4
        NQ = TILES // GQ
        V = 28
        g_gcol = sb("g_gcol", [P, GQ])
        g_XT = theta_tok[:, :, :].rearrange("p j c -> p (j c)").rearrange("p (k n) -> p k n", k=KC)
        w2_flat = w2_sb[:, :, :, :].rearrange("p e f c -> p (e f c)")
        size = 2 * KC * FFN
        g_w1 = w2_flat[:, 0:size].rearrange("p (s k f) -> p s k f", s=2, k=KC)
        g_w2 = w2_flat[:, size:2 * size].rearrange("p (s f c) -> p s f c", s=2, f=FC)
        g_h = w1_got[:, :, :].rearrange("p d f -> p (d f)").rearrange("p (f n) -> p f n", f=FC)
        g_acc = x_sb

        bank = [psum(f"bank{i}", [P, 512]) for i in range(8)]

        consts = sem("consts")
        masks = sem("masks")
        ones_set = sem("ones_set")
        slot1_set = sem("slot1_set")
        cleared = sem("cleared")
        small_in = sem("small_in")
        x_in = [sem(f"x_in{i}") for i in range(XG)]
        w2_in = [sem(f"w2_in{i}") for i in range(E)]
        copied = sem("copied")
        vec = sem("vec")
        theta_set = sem("theta_set")
        thetas = sem("thetas")
        theta_out = sem("theta_out")
        router_t = sem("router_t")
        router_out = sem("router_out")
        router3_set = sem("router3_set")
        rates = sem("rates")
        x_seen = sem("x_seen")
        counted = sem("counted")
        cums = sem("cums")
        floored = sem("floored")
        diffs = sem("diffs")
        act_set = sem("act_set")
        info_set = sem("info_set")
        prefixed = sem("prefixed")
        slots_set = sem("slots_set")
        slotted = sem("slotted")
        slotted2 = sem("slotted2")
        pair_at_set = sem("pair_at_set")
        pairs_mapped = sem("pairs_mapped")
        compactT = sem("compactT")
        spikesT_out = sem("spikesT_out")
        spikesT_out2 = sem("spikesT_out2")
        informed = sem("informed")
        keyed_mm = sem("keyed_mm")
        logits = sem("logits")
        shift_set = sem("shift_set")
        exps = sem("exps")
        chose = sem("chose")
        ranked = sem("ranked")
        routes = sem("routes")
        placed = sem("placed")
        maps_set = sem("maps_set")
        info_set2 = sem("info_set2")
        mapped = sem("mapped")
        info_out = sem("info_out")
        map_out = sem("map_out")
        w2_hi_set = sem("w2_hi_set")
        w2_lo_set = [sem(f"w2_lo_set{e}") for e in range(E)]
        h_lo_set = sem("h_lo_set")
        y_hi_set = sem("y_hi_set")
        y_lo_set = sem("y_lo_set")
        combined = sem("combined")
        out_set = sem("out_set")
        y_ready = sem("y_ready")
        few_in = sem("few_in")
        indexed = sem("indexed")
        pair_mm = sem("pair_mm")
        paired = sem("paired")
        w1_in = [sem(f"w1_in{i}") for i in range(D)]
        h_ready = sem("h_ready")
        h_done = sem("h_done")
        y_set = sem("y_set")
        added = sem("added")
        summed_up = sem("summed_up")
        verdict_mm = sem("verdict_mm")
        verdict_set = sem("verdict_set")

        warm_set = sem("warm_set")
        warmed = sem("warmed")

        turned = sem("turned")
        turned_out = sem("turned_out")
        gx_in = sem("gx_in")
        g_vec = sem("g_vec")
        g_rates = sem("g_rates")
        g_cums = sem("g_cums")
        g_xts = sem("g_xts")
        g_logits = sem("g_logits")
        g_max = sem("g_max")
        g_exps = sem("g_exps")
        g_hot = sem("g_hot")
        g_ranks = sem("g_ranks")
        g_routed = sem("g_routed")
        w_in = [sem("w_in0"), sem("w_in1")]
        h_mm = sem("h_mm")
        h_act = sem("h_act")
        y_mm = sem("y_mm")
        y_add = sem("y_add")
        out_done = sem("out_done")

        CUM = [bank[i] for i in range(3)]
        DIF = [bank[3 + i] for i in range(3)]
        TH = [bank[6 + i] for i in range(2)]
        within_ps = bank[7][:, 32:32 + TILES]
        total_ps_s = bank[7][:, 64:64 + TILES]
        slotsT_ps = [bank[k][:, 0:SLOTS] for k in range(KC)]
        info_ps = bank[6][:, 32:32 + ST * 3].rearrange("p (t i) -> p t i", t=ST)
        keyed_ps = [bank[2 + t][:, 0:H] for t in range(ST)]
        logit_s = bank[4][:, 0:ST * E].rearrange("p (t e) -> p t e", t=ST)
        rank_ps_s = bank[5][:, 0:ST * 2 * E].rearrange("p (t e) -> p t e", t=ST)
        place_ps = bank[4][:, 64:64 + ST * 2 * E].rearrange("p (t e) -> p t e", t=ST)
        pair_ps = bank[0][:, 32:32 + PI * E].rearrange("p (e i) -> p e i", e=E)
        verdict_ps = bank[6][0:1, 0:1]
        MAP = [bank[i][:, 0:INFO] for i in (0, 1, 6, 7)]
        OUT = [bank[t][:, 0:H] for t in range(ST)]
        HID = [[bank[2], bank[3]], [bank[4], bank[5]]]
        Y = [bank[6][:, 0:H], bank[7][:, 0:H]]

        csum = bank[0][:, 0:KC * P].rearrange("p (k n) -> p k n", k=KC)
        logit = bank[1][:, 0:E]
        rank_ps = bank[2][:, 0:TOP_K * E]
        total_ps = bank[3][:, 0:TOP_K * E]

        block = ctx.enter_context(nc.Block())

        @block.sync
        def _(sp):
            sp.dma_start(cond3[:, :], cond.unsqueeze(0).to_broadcast([3, B, H])).then_inc(small_in, 16)
            for g in range(XG):
                sp.dma_start(x_sb[:, 2 * g:2 * g + 2, :], x_tiles[:, 2 * g:2 * g + 2, :]).then_inc(x_in[g], 16)
            for e in range(E):
                if e >= WR:
                    sp.wait_ge(w2_lo_set[e - WR], 1)
                sp.dma_start(w2_sb[:, e % WR, :, :], w2[e].rearrange("(f p) c -> p f c", p=P)).then_inc(w2_in[e], 16)
                if e == 1:
                    for g in range(XG):
                        sp.wait_ge(x_in[g], 16)
                    sp.dma_start(out_tiles, x_sb[:, :, :]).then_inc(copied, 16)
            sp.wait_ge(copied, 16)
            sp.wait_ge(added, 16 * ST)

            sp.wait_ge(verdict_set, 1)
            with sp.If(sp.value_load(verdict[0:1, 0:1]) != P * NV):
                with sp.Fori(0, TILES) as j:
                    sp.wait_ge(g_rates, j + 1)
                    sp.dma_start(g_x[:, :], x_tiles[:, bass.ds(j, 1), :].rearrange("p a c -> p (a c)")).then_inc(gx_in, 16)
                with sp.Fori(0, E // 2) as pair:
                    for side in range(2):
                        e = pair * 2 + side
                        sp.wait_ge(y_mm, pair * (2 * NQ) + 1)
                        sp.dma_start(g_w1[:, side, :, :], w1[bass.ds(e, 1), :, :].rearrange("e (k p) f -> p (e k) f", p=P)).then_inc(w_in[side], 16)
                        sp.dma_start(g_w2[:, side, :, :], w2[bass.ds(e, 1), :, :].rearrange("e (k p) c -> p (e k) c", p=P)).then_inc(w_in[side], 16)
                sp.wait_ge(y_add, E * NQ * GQ + 1)
                sp.dma_start(out_tiles, g_acc[:, :, :]).then_inc(out_done, 16)
                sp.wait_ge(out_done, 16)

        @block.gpsimd
        def _(pool):
            g = nc.gpsimd
            g.memset(ones_b[:, :], 1.0).then_inc(ones_set, 1)
            g.memset(ident3[:, :], 0.0).then_inc(consts, 1)
            g.memset(cum_seq[:, :], 1.0).then_inc(consts, 1)
            g.memset(step_seq[:, :], 0.0).then_inc(consts, 1)
            g.memset(cum_tile[:, :], 1.0).then_inc(consts, 1)
            g.memset(ident[:, :], 0.0).then_inc(consts, 1)
            pool.wait_ge(consts, 5)
            for i in range(3):
                g.affine_select(out=ident3[i * B:(i + 1) * B, :], in_=ident3[i * B:(i + 1) * B, :],
                                compare_op=ALU.not_equal, fill=1.0, base=0, pattern=[[-1, B]],
                                channel_multiplier=1).then_inc(masks, 1)
            pool.wait_ge(masks, 3)
            for m in (cum_seq, cum_tile):
                g.affine_select(out=m[:, :], in_=m[:, :], compare_op=ALU.is_ge, fill=0.0, base=0,
                                pattern=[[1, P]], channel_multiplier=-1).then_inc(consts, 1)
            g.affine_select(out=step_seq[:, :], in_=step_seq[:, :], compare_op=ALU.not_equal, fill=1.0, base=0,
                            pattern=[[-1, P]], channel_multiplier=1).then_inc(consts, 1)
            pool.wait_ge(consts, 8)
            g.memset(cum_seq[0:T, T:P], 0.0).then_inc(masks, 1)
            g.affine_select(out=step_seq[:, :], in_=step_seq[:, :], compare_op=ALU.not_equal, fill=-1.0, base=1,
                            pattern=[[-1, P]], channel_multiplier=1).then_inc(consts, 1)
            pool.wait_ge(consts, 9)
            g.memset(step_seq[0:T, T:P], 0.0).then_inc(masks, 1)
            g.affine_select(out=ident[:, :], in_=ident[:, :], compare_op=ALU.not_equal, fill=1.0, base=0,
                            pattern=[[-1, P]], channel_multiplier=1).then_inc(masks, 1)

            def numbers(out, pattern, base=0, step=0):
                return g.iota(out, pattern, base=base, channel_multiplier=step,
                              allow_small_or_imprecise_dtypes=True)

            g.memset(zeros_b[:, :], 0.0).then_inc(masks, 1)
            numbers(slot1[:, :], [[1, SLOTS]], 1).then_inc(slot1_set, 1)
            numbers(spikes[:, :, H], [[0, TILES]], step=1).then_inc(masks, 1)
            numbers(spikes[:, :, H + 1], [[1, TILES]]).then_inc(masks, 1)
            g.memset(carry[:, :], 1.0).then_inc(masks, 1)
            g.memset(x_bound[:, :], -X_MAX).then_inc(masks, 1)
            g.memset(before[:, 0:1], 0.0).then_inc(masks, 1)
            numbers(place[:, :], [[1, EVENTS]]).then_inc(masks, 1)
            numbers(eight[:, :], [[1, JM]]).then_inc(masks, 1)
            numbers(part[:, :], [[0, 1]], step=1).then_inc(masks, 1)
            numbers(slot_no[:, :], [[P, ST]], step=1).then_inc(masks, 1)
            numbers(desc[:, :], [[-1, E]], E).then_inc(masks, 1)
            g.memset(first_two[:, :], 0.0).then_inc(consts, 1)
            g.memset(faults[:, 1:2], 0.0).then_inc(masks, 1)
            for e in range(E):
                g.memset(slot_map[:, :, e, INFO - 1:INFO], float(e % 2 * H) - FAR).then_inc(masks, 1)
            pool.wait_ge(consts, 10)
            g.memset(first_two[:, 0:1], 1.0).then_inc(masks, 1)
            g.memset(first_two[:, E + 1:E + 2], 1.0).then_inc(masks, 1)
            pool.wait_ge(slot1_set, 1)
            for k in range(KC):
                g.affine_select(out=key_diag[:, k, :], in_=slot1[:, k * P:(k + 1) * P], compare_op=ALU.is_equal,
                                fill=0.0, base=0, pattern=[[-1, P]], channel_multiplier=1).then_inc(masks, 1)
            for d in range(D):
                g.memset(w1_got[:, d, :], 0.0).then_inc(cleared, 1)
            pool.wait_ge(cleared, D)
            pool.wait_ge(slots_set, 2)
            for j in range(TILES - POOL_TILES, TILES):
                g.tensor_scalar(to_slot[:, j, :], slot1[:, :], slot_of[:, j:j + 1], None, ALU.is_equal).then_inc(slotted2, 1)

            def split_w2(e):
                pool.wait_ge(w2_hi_set, e + 1)
                if e >= 2:
                    pool.wait_ge(y_ready, e - 1)
                g.tensor_tensor(w2_lo[:, e % 2, :, :], w2_sb[:, e % WR, :, :], w2_hi[:, e % 3, :, :],
                                ALU.subtract).then_inc(w2_lo_set[e], 1)

            def map_pairs(e):
                for t in range(ST):
                    ins = g.tensor_scalar(slot_map[:, t, e, 0:PAIRS], slot1[:, 0:PAIRS], pair_at[:, t, e:e + 1],
                                          None, ALU.is_equal)
                ins.then_inc(pairs_mapped, 1)

            def gather(d):
                pool.wait_ge(indexed, d + 1)
                g.indirect_dma_start(
                    out=w1_got[:, d, :], out_offset=None, in_=w1_rows[:, :],
                    in_offset=bass.IndirectOffsetOnAxis(ap=w1_index[:, d:d + 1], axis=0),
                    bounds_check=E * H - 1, oob_is_err=False, compute_op=ALU.bypass).then_inc(w1_in[d], 16)

            split_w2(0)
            pool.wait_ge(pair_at_set, 1)
            for e in range(1, 4):
                map_pairs(e)
            gather(0)
            map_pairs(4)
            map_pairs(5)
            gather(1)
            map_pairs(6)
            gather(2)
            gather(3)
            split_w2(3)
            split_w2(5)
            pool.wait_ge(copied, 16)
            for t in range(ST):
                pool.wait_ge(out_set, t + 1)
                g.indirect_dma_start(
                    out=out_rows[:, :], out_offset=bass.IndirectOffsetOnAxis(ap=out_index[:, t:t + 1], axis=0),
                    in_=ffn_out[:, t, :], in_offset=None, bounds_check=N - 1, oob_is_err=False,
                    compute_op=ALU.add).then_inc(added, 16)
            pool.wait_ge(added, 16 * ST)
        MASKS = 30

        @block.tensor
        def _(pe):
            def keep_warm(n):
                for _ in range(n):
                    nc.tensor.matmul(bank[2][:, 0:4 * P], ones_b[:, :],
                                     ones_b[:, :].unsqueeze(1).to_broadcast([P, 4, P]), start=True, stop=True)

            def spread_theta(g):
                if g >= 2:
                    pe.wait_ge(theta_out, g - 1)
                for i in range(2):
                    j = 2 * g + i
                    mm = nc.tensor.matmul(TH[g % 2][:, i * H:(i + 1) * H],
                                          spread[:, BPT * j:BPT * (j + 1), :].rearrange("k b t -> k (b t)"),
                                          theta3[:, :], start=True, stop=True)
                mm.then_inc(thetas, 1)

            def cumulate(g):
                pe.wait_ge(rates, g + 1)
                if g >= 3:
                    pe.wait_ge(floored, g - 2)
                nc.tensor.matmul(CUM[g % 3][:, 0:GW], cum_seq[:, :],
                                 rate[:, g % RING, :, :].rearrange("p j c -> p (j c)"),
                                 start=True, stop=True).then_inc(cums, 1)

            def difference(g):
                pe.wait_ge(floored, g + 1)
                if g == 2:
                    pe.wait_ge(router_out, 1)
                if g >= 3:
                    pe.wait_ge(counted, 2 * (g - 2))
                nc.tensor.matmul(DIF[g % 3][:, 0:GW], step_seq[:, :],
                                 floors[:, g % RING, :, :].rearrange("p j c -> p (j c)"),
                                 start=True, stop=True).then_inc(diffs, 1)

            def count_active(part):
                lo, hi = PARTS[part]
                pe.wait_ge(act_set, part + 1)
                pe.wait_ge(masks, MASKS)
                if part == 0:
                    pe.wait_ge(theta_out, XG)
                nc.tensor.matmul(within_ps[:, lo:hi], cum_tile[:, :], active[:, lo:hi], start=True, stop=True)
                nc.tensor.matmul(total_ps_s[:, lo:hi], ones_b[:, :], active[:, lo:hi], start=True, stop=True).then_inc(prefixed, 1)

            pe.wait_ge(ones_set, 1)
            keep_warm(WARM_START)
            pe.wait_ge(few_in, 16)
            pe.wait_ge(masks, 6)
            for k in range(KC):
                mm = nc.tensor.transpose(bank[5][:, k * E:(k + 1) * E], router_rows[:, k * P:(k + 1) * P], ident[0:E, 0:E])
            mm.then_inc(router_t, 1)
            keep_warm(3)
            pe.wait_ge(theta_set, 1)
            spread_theta(0)
            for g in range(XG):
                cumulate(g)
                if g == 0:
                    spread_theta(1)
                if g + 2 < XG:
                    spread_theta(g + 2)
                if g:
                    difference(g - 1)
            count_active(0)
            difference(XG - 1)
            def compact_tile(j):
                if j < TILES - POOL_TILES:
                    pe.wait_ge(slotted, j + 1)
                else:
                    pe.wait_ge(slotted2, j + 1 - (TILES - POOL_TILES))
                for k in range(KC):
                    mm = nc.tensor.matmul(slotsT_ps[k], spikes[:, j, k * P:(k + 1) * P], to_slot[:, j, :],
                                          start=(j == 0), stop=(j == TILES - 1))
                return mm

            for j in range(4):
                compact_tile(j)
            count_active(1)
            for j in range(4, TILES):
                mm = compact_tile(j)
            mm.then_inc(compactT, 1)
            pe.wait_ge(router3_set, 1)
            pe.wait_ge(info_set, len(PARTS))
            def take_info(t):
                for j in range(TILES):
                    mm = nc.tensor.matmul(info_ps[:, t, :], to_slot[:, j, t * P:(t + 1) * P], spikes[:, j, H:H + 3],
                                          start=(j == 0), stop=(j == TILES - 1))
                mm.then_inc(informed, 1)

            take_info(0)
            pe.wait_ge(spikesT_out, 1)
            pe.wait_ge(spikesT_out2, 1)
            for t in range(ST):
                for i, k in ((i, k) for i in range(3) for k in range(KC)):
                    mm = nc.tensor.matmul(logit_s[:, t, :], spikesT[:, k, t * P:(t + 1) * P], router3[:, i, k, :],
                                          start=(i == 0 and k == 0), stop=(i == 2 and k == KC - 1))
            mm.then_inc(logits, 1)
            take_info(1)
            for t in range(ST):
                for k in range(KC):
                    mm = nc.tensor.matmul(keyed_ps[t][:, k * P:(k + 1) * P], spikesT[:, k, t * P:(t + 1) * P],
                                          key_diag[:, k, :], start=True, stop=True)
            mm.then_inc(keyed_mm, 1)

            def count_slots(dst, src):
                for t in range(ST):
                    mm = nc.tensor.matmul(dst[:, t, :], cum_tile[:, :], src[:, t, :], start=True, stop=(t == 0))
                    for before_t in range(t):
                        mm = nc.tensor.matmul(dst[:, t, :], ones_b[:, :], src[:, before_t, :],
                                              start=False, stop=(before_t == t - 1))
                return mm

            pe.wait_ge(chose, TOP_K)
            count_slots(rank_ps_s, chosen).then_inc(ranked, 1)
            nc.tensor.matmul(place_ps[:, 0, :], ones_b[:, :], zeros_b[:, :], start=True, stop=False)
            pe.wait_ge(routes, 1)
            for t in range(ST):
                if t:
                    nc.tensor.matmul(place_ps[:, t, :], ones_b[:, :], routed[:, 0, :], start=True, stop=False)
                for u in range(ST):
                    nc.tensor.matmul(place_ps[:, t, 1::2], ones_b[:, :], routed[:, u, 0::2],
                                     start=False, stop=False, skip_group_check=True)
                mm = nc.tensor.matmul(place_ps[:, t, :], cum_tile[:, :], routed[:, t, :], start=False, stop=True)
            mm.then_inc(placed, 1)

            def make_map(d):
                n = 0
                for e in (2 * d, 2 * d + 1):
                    pe.wait_ge(maps_set, e + 1)
                    if 0 < e < E - 1:
                        pe.wait_ge(pairs_mapped, e)
                    for edge in (from_start, from_end):
                        for t in range(ST):
                            mm = nc.tensor.matmul(MAP[d], edge[:, t, e, :], slot_map[:, t, e, :],
                                                  start=(n == 0), stop=(n == 4 * ST - 1))
                            n += 1
                mm.then_inc(mapped, 1)

            def take_pairs():
                pe.wait_ge(info_set2, 1)
                for e in range(E):
                    for t in range(ST):
                        mm = nc.tensor.matmul(pair_ps[:, e, :], slot_map[:, t, e, 0:PAIRS], pair_info[:, t, :, e],
                                              start=(t == 0), stop=(t == ST - 1))
                mm.then_inc(pair_mm, 1)

            def hidden(d):
                pe.wait_ge(w1_in[d], 16)
                pe.wait_ge(map_out, d + 1)
                for half in range(2):
                    if d >= 2:
                        pe.wait_ge(h_done, 4 * (d - 2) + 2 + half + 1)
                    for i in range(CH):
                        f = half * CH + i
                        mm = nc.tensor.matmul(HID[d % 2][half][:, i * PAIRS:(i + 1) * PAIRS],
                                              w1_got[:, d, f * P:(f + 1) * P], ev_pair[:, d, :], start=True, stop=True)
                    mm.then_inc(h_ready, 1)

            def project(e):
                d = e // 2
                if e >= 2:
                    pe.wait_ge(y_set, e - 1)
                    if e % 2:
                        pe.wait_ge(y_hi_set, d)
                else:
                    pe.wait_ge(map_out, 3 + e)
                pe.wait_ge(w2_hi_set, e + 1)
                for f in range(FC):
                    if f % CH == 0:
                        pe.wait_ge(h_done, 4 * d + f // CH + 1)
                    nc.tensor.matmul(Y[e % 2], hT_hi[:, d % 2, f, :], w2_hi[:, e % 3, f, :],
                                     start=(f == 0), stop=False)
                pe.wait_ge(w2_lo_set[e], 1)
                for f in range(FC):
                    nc.tensor.matmul(Y[e % 2], hT_hi[:, d % 2, f, :], w2_lo[:, e % 2, f, :],
                                     start=False, stop=False)
                for f in range(FC):
                    if f % CH == 0:
                        pe.wait_ge(h_lo_set, 2 * d + f // CH + 1)
                    mm = nc.tensor.matmul(Y[e % 2], hT_lo[:, d % 2, f, :], w2_hi[:, e % 3, f, :],
                                          start=False, stop=(f == FC - 1))
                mm.then_inc(y_ready, 1)

            def combine(d):
                pe.wait_ge(paired, d + 1)
                if d == D - 1:
                    pe.wait_ge(y_set, 2 * d + 2)
                    for t in range(ST):
                        nc.tensor.matmul(OUT[t], to_out[:, d, t * P:(t + 1) * P].bitcast(F32), y[:, d % 2, :],
                                         start=False, stop=True).then_inc(combined, 1)
                    return
                pe.wait_ge(y_hi_set, d + 1)
                for t in range(ST):
                    nc.tensor.matmul(OUT[t], to_out[:, d, t * P:(t + 1) * P], y_hi[:, d % 2, :],
                                     start=(d == 0), stop=False)
                pe.wait_ge(y_lo_set, d + 1)
                for t in range(ST):
                    nc.tensor.matmul(OUT[t], to_out[:, d, t * P:(t + 1) * P], y_lo[:, d % 2, :],
                                     start=False, stop=False).then_inc(combined, 1)

            for d in range(D - 1):
                make_map(d)
                keep_warm(WARM[d])
            hidden(0)
            make_map(D - 1)
            project(0)
            take_pairs()
            for d in range(D):
                if d + 1 < D:
                    hidden(d + 1)
                if d:
                    combine(d - 1)
                project(2 * d + 1)
                if d + 1 < D:
                    project(2 * d + 2)
            combine(D - 1)
            pe.wait_ge(summed_up, 1)
            nc.tensor.matmul(verdict_ps, fine_sum[:, :], carry_f[:, :], start=True, stop=True).then_inc(verdict_mm, 1)

            pe.wait_ge(added, 16 * ST)
            pe.wait_ge(verdict_set, 1)
            with pe.If(pe.value_load(verdict[0:1, 0:1]) != P * NV):
                pe.sem_inc(y_mm, 1)
                for k in range(KC):
                    mm = nc.tensor.transpose(bank[0][:, k * B:(k + 1) * B], cond3[0:B, k * P:(k + 1) * P], ident[0:B, 0:B])
                mm.then_inc(turned, 1)
                pe.wait_ge(turned_out, 1)
                with pe.Fori(0, TILES) as j:
                    pe.wait_ge(g_rates, j + 2)
                    for k in range(KC):
                        mm = nc.tensor.matmul(csum[:, k, :], g_rate[:, k * P:(k + 1) * P], cum_seq[:, :], start=True, stop=True)
                    mm.then_inc(g_cums, 1)
                    pe.wait_ge(g_xts, j + 1)
                    for k in range(KC):
                        mm = nc.tensor.matmul(logit, g_xt[:, k, :], routerT[:, k, :], start=(k == 0), stop=(k == KC - 1))
                    mm.then_inc(g_logits, 1)
                    pe.wait_ge(g_hot, j + 1)
                    nc.tensor.matmul(rank_ps, cum_tile[:, :], g_oh[:, :], start=True, stop=True)
                    nc.tensor.matmul(total_ps, ones_b[:, :], g_oh[:, :], start=True, stop=True).then_inc(g_ranks, 1)
                pe.wait_ge(g_routed, 1)
                with pe.Fori(0, E // 2) as pair:
                    for side in range(2):
                        with pe.Fori(0, NQ) as q:
                            step = (pair * 2 + side) * NQ + q
                            pe.wait_ge(w_in[side], pair * 32 + 32)
                            for f in range(FC):
                                if f < 2:
                                    pe.wait_ge(h_act, step * FC + 1)
                                else:
                                    pe.wait_ge(h_act, step * FC + f)
                                for k in range(KC):
                                    mm = nc.tensor.matmul(bank[f % 2][:, 0:GQ * P], g_w1[:, side, k, f * P:(f + 1) * P],
                                                          g_XT[:, k, bass.ds(q * (GQ * P), GQ * P)],
                                                          start=(k == 0), stop=(k == KC - 1))
                                mm.then_inc(h_mm, 1)
                            pe.wait_ge(h_act, step * FC + FC + 1)
                            pe.wait_ge(y_add, step * GQ + 1)
                            for s in range(GQ):
                                for f in range(FC):
                                    mm = nc.tensor.matmul(bank[2 + s][:, 0:H], g_h[:, f, s * P:(s + 1) * P], g_w2[:, side, f, :],
                                                          start=(f == 0), stop=(f == FC - 1))
                            mm.then_inc(y_mm, 1)

        @block.scalar
        def _(act):
            act.dma_start(router_rows[:, :], router_w).then_inc(few_in, 16)

            def take_theta(g):
                act.wait_ge(thetas, g + 1)
                nc.scalar.copy(theta_tok[:, 2 * g:2 * g + 2, :].rearrange("p j c -> p (j c)"), TH[g % 2][:, 0:GW]).then_inc(theta_out, 1)

            def take_spikes(g):
                act.wait_ge(diffs, g + 1)
                for i in range(2):
                    j = 2 * g + i
                    nc.scalar.activation(spikes[:, j, 0:H], DIF[g % 3][:, i * H:(i + 1) * H], ACT.Copy,
                                         accum_out=count[:, j:j + 1]).then_inc(counted, 1)

            for g in range(XG):
                take_theta(g)
                if g >= 3:
                    take_spikes(g - 3)
            for g in range(XG - 3, XG):
                take_spikes(g)
            act.wait_ge(warm_set, 1)
            nc.scalar.activation(warm[:, 1:2], warm[:, 0:1], ACT.Exp).then_inc(warmed, 1)
            def round_w2(e):
                act.wait_ge(w2_in[e], 16)
                if e >= 3:
                    act.wait_ge(y_ready, e - 2)
                nc.scalar.copy(w2_hi[:, e % 3, :, :], w2_sb[:, e % WR, :, :]).then_inc(w2_hi_set, 1)

            def take_map(d):
                act.wait_ge(info_out, d + 1)
                nc.scalar.copy(ev_pair[:, d, :], MAP[d][:, 0:PAIRS]).then_inc(map_out, 1)

            def gelu(d):
                if d >= 2:
                    act.wait_ge(y_ready, 2 * (d - 1))
                for dst in (hT_hi, hT):
                    for half in range(2):
                        act.wait_ge(h_ready, 2 * d + half + 1)
                        nc.scalar.activation(dst[:, d % 2, half * CH:(half + 1) * CH, :].rearrange("p f n -> p (f n)"),
                                             HID[d % 2][half][:, 0:CH * PAIRS], ACT.Gelu, scale=SPIKE).then_inc(h_done, 1)

            round_w2(0)
            round_w2(1)
            act.wait_ge(compactT, 1)
            nc.scalar.copy(spikesT[:, 0, :], slotsT_ps[0]).then_inc(spikesT_out, 1)
            act.wait_ge(shift_set, 1)
            nc.scalar.activation(expo[:, :, :], shifted[:, :, :], ACT.Exp).then_inc(exps, 1)
            act.wait_ge(warmed, 1)
            nc.scalar.activation(warm[:, 2:3], warm[:, 0:1], ACT.Gelu).then_inc(warmed, 1)
            round_w2(2)
            act.wait_ge(informed, ST)
            act.wait_ge(masks, MASKS)
            nc.scalar.activation(to_slot[:, :, :].rearrange("p j s -> p (j s)"), x_sb[:, :, :].rearrange("p j c -> p (j c)"),
                                 ACT.Relu, bias=x_bound[:, 0:1], accum_out=faults[:, 0:1]).then_inc(x_seen, 1)
            for d in range(D - 1):
                take_map(d)
            gelu(0)
            take_map(D - 1)
            round_w2(3)
            gelu(1)
            round_w2(4)
            round_w2(5)
            gelu(2)
            round_w2(6)
            round_w2(7)
            gelu(3)
            for t in range(ST):
                act.wait_ge(combined, ST * (D - 1) + t + 1)
                nc.scalar.copy(ffn_out[:, t, :], OUT[t]).then_inc(out_set, 1)

            act.wait_ge(added, 16 * ST)
            act.wait_ge(verdict_set, 1)
            with act.If(act.value_load(verdict[0:1, 0:1]) != P * NV):
                act.sem_inc(h_act, 1)
                with act.Fori(0, TILES) as j:
                    act.wait_ge(g_max, j + 1)
                    nc.scalar.activation(g_e[:, :], logit, ACT.Exp, bias=g_one[:, 1:2]).then_inc(g_exps, 1)
                with act.Fori(0, E * NQ) as step:
                    for f in range(FC):
                        act.wait_ge(h_mm, step * FC + f + 1)
                        if f == 0:
                            act.wait_ge(y_mm, step + 1)
                        nc.scalar.activation(g_h[:, f, :], bank[f % 2][:, 0:GQ * P], ACT.Gelu).then_inc(h_act, 1)

        @block.vector
        def _(dve):
            v = nc.vector
            steps = [0]

            def link(ins):
                steps[0] += 1
                ins.then_inc(vec, 1)
                dve.wait_ge(vec, steps[0])

            def loose(ins):
                steps[0] += 1
                ins.then_inc(vec, 1)

            v.memset(warm[:, 0:1], 0.0).then_inc(warm_set, 1)
            loose(v.memset(carry_f[:, :], 1.0))
            dve.wait_ge(masks, 3)
            loose(v.tensor_copy(spread[:, :, :], ident3[:, :].unsqueeze(2).to_broadcast([3 * B, B, T])))
            dve.wait_ge(small_in, 16)
            link(v.tensor_scalar(theta[:, :], cond3[:, :], -1.0, 1.0, ALU.mult, ALU.add))
            link(v.tensor_scalar(theta[:, :], theta[:, :], -HALF_ULP, None, ALU.add))
            link(v.tensor_copy(theta3[:, :], theta[:, :]))
            link(v.tensor_tensor(theta_r[:, :], theta[:, :], theta3[:, :], ALU.subtract))
            link(v.tensor_copy(theta_mid[:, :], theta_r[:, :]))
            loose(v.tensor_copy(theta3[B:2 * B, :], theta_mid[B:2 * B, :]))
            v.tensor_tensor(theta3[2 * B:, :], theta_r[2 * B:, :], theta_mid[2 * B:, :], ALU.subtract).then_inc(theta_set, 1)

            def take_rates(g):
                dve.wait_ge(x_in[g], 16)
                v.tensor_scalar(rate[:, g % RING, :, :], x_sb[:, 2 * g:2 * g + 2, :], 0.0, float(DT),
                                ALU.max, ALU.mult).then_inc(rates, 1)

            def mark_active(part):
                lo, hi = PARTS[part]
                dve.wait_ge(counted, hi)
                v.tensor_scalar(active[:, lo:hi], count[:, lo:hi], 0.5, None, ALU.is_gt).then_inc(act_set, 1)
                v.tensor_copy(spikes[:, lo:hi, H + 2], count[:, lo:hi]).then_inc(info_set, 1)

            def take_slots(part, maps=()):
                lo, hi = PARTS[part]
                dve.wait_ge(act_set, part + 1)
                dve.wait_ge(masks, MASKS)
                dve.wait_ge(prefixed, part + 1)
                loose(v.tensor_tensor_scan(before[:, lo + 1:hi + 1], carry[:, lo:hi], total_ps_s[:, lo:hi],
                                           before[:, lo:lo + 1] if part else 0.0, ALU.mult, ALU.add))
                for j in maps[0:1]:
                    map_slots(j)
                dve.wait_ge(vec, steps[0])
                loose(v.tensor_tensor(rank_t[:, lo:hi], within_ps[:, lo:hi], before[:, lo:hi], ALU.add))
                for j in maps[1:2]:
                    map_slots(j)
                dve.wait_ge(vec, steps[0])
                v.tensor_tensor(slot_of[:, lo:hi], rank_t[:, lo:hi], active[:, lo:hi], ALU.mult).then_inc(slots_set, 1)
                for j in maps[2:3]:
                    map_slots(j)
                dve.wait_ge(slots_set, part + 1)

            def map_slots(j):
                v.tensor_scalar(to_slot[:, j, :], slot1[:, :], slot_of[:, j:j + 1], None, ALU.is_equal).then_inc(slotted, 1)

            take_rates(0)
            take_rates(1)
            dve.wait_ge(router_t, 1)
            v.tensor_copy(routerT[:, :, :], bank[5][:, 0:KC * E].rearrange("p (k e) -> p k e", k=KC)).then_inc(router_out, 1)
            for g in range(XG):
                dve.wait_ge(cums, g + 1)
                dve.wait_ge(theta_out, g + 1)
                if g >= RING:
                    dve.wait_ge(diffs, g - RING + 1)
                v.tensor_tensor(floors[:, g % RING, :, :].rearrange("p j c -> p (j c)"), CUM[g % 3][:, 0:GW],
                                theta_tok[:, 2 * g:2 * g + 2, :].rearrange("p j c -> p (j c)"), ALU.is_ge).then_inc(floored, 1)
                if g + 2 < XG:
                    take_rates(g + 2)
                dve.wait_ge(vec, steps[0])
                if g == 0:
                    dve.wait_ge(router_out, 1)
                    loose(v.tensor_scalar(router_s[:, :, :], routerT[:, :, :], SPIKE, None, ALU.mult))
                if g == 1:
                    loose(v.tensor_copy(router3[:, 0, :, :], router_s[:, :, :]))
                if g == 2:
                    loose(v.tensor_tensor(router_r[:, :, :], router_s[:, :, :], router3[:, 0, :, :], ALU.subtract))
                if g == 3:
                    loose(v.tensor_copy(router3[:, 1, :, :], router_r[:, :, :]))
                if g == 4:
                    v.tensor_tensor(router3[:, 2, :, :], router_r[:, :, :], router3[:, 1, :, :], ALU.subtract).then_inc(router3_set, 1)
                if g == XG - 2:
                    mark_active(0)

            take_slots(0)
            for j in range(4):
                map_slots(j)
            mark_active(1)
            for j in range(4, 7):
                map_slots(j)
            take_slots(1, maps=(7, 8, 9))
            for j in range(10, TILES - POOL_TILES):
                map_slots(j)
            loose(v.tensor_scalar(unused[:, :], slot_no[:, :], before[:, TILES:TILES + 1], FAR, ALU.is_ge, ALU.mult))

            dve.wait_ge(compactT, 1)
            v.tensor_copy(spikesT[:, 1, :], slotsT_ps[1]).then_inc(spikesT_out2, 1)
            dve.wait_ge(logits, 1)
            link(v.tensor_reduce(top_l[:, :], logit_s, AX_X, ALU.max))
            v.tensor_tensor(shifted[:, :, :], logit_s, top_l[:, :].unsqueeze(2).to_broadcast([P, ST, E]),
                            ALU.subtract).then_inc(shift_set, 1)
            dve.wait_ge(informed, ST)
            loose(v.tensor_copy(slot_info[:, :, :], info_ps))
            dve.wait_ge(exps, 1)
            for t in range(ST):
                loose(v.max(best[:, t, :], expo[:, t, :]))
            dve.wait_ge(vec, steps[0] - ST)
            loose(v.scalar_tensor_tensor(token_no[:, :], slot_info[:, :, 1], float(P), slot_info[:, :, 0], ALU.mult, ALU.add))
            dve.wait_ge(vec, steps[0] - 1)
            for t in range(ST):
                loose(v.max_index(best_at[:, t, :], best[:, t, :], expo[:, t, :]))
            dve.wait_ge(vec, steps[0] - ST)
            loose(v.tensor_tensor(inactive[:, :], token_no[:, :], slot_no[:, :], ALU.subtract))
            dve.wait_ge(vec, steps[0] - 1)
            for k in range(TOP_K):
                v.tensor_tensor(chosen[:, :, k * E:(k + 1) * E], eight[:, :].unsqueeze(1).to_broadcast([P, ST, E]),
                                best_at[:, :, k].unsqueeze(2).to_broadcast([P, ST, E]), ALU.is_equal).then_inc(chose, 1)
            dve.wait_ge(vec, steps[0])
            for t in range(ST):
                loose(v.tensor_scalar(base[:, t, :], first_two[:, :], inactive[:, t:t + 1], unused[:, t:t + 1], ALU.mult, ALU.add))

            dve.wait_ge(chose, TOP_K)
            dve.wait_ge(ranked, 1)
            dve.wait_ge(vec, steps[0])
            link(v.tensor_tensor(rank_s[:, :, :], rank_ps_s, base[:, :, :], ALU.add))
            link(v.scalar_tensor_tensor(kept[:, :, :], rank_s[:, :, :], float(CAP), chosen[:, :, :], ALU.is_le, ALU.mult))
            link(v.tensor_tensor(routed[:, :, 0:E], kept[:, :, 0:E], kept[:, :, E:2 * E], ALU.add))
            v.tensor_tensor(routed[:, :, E:2 * E], routed[:, :, 0:E],
                            slot_info[:, :, 2].unsqueeze(2).to_broadcast([P, ST, E]), ALU.mult).then_inc(routes, 1)
            dve.wait_ge(keyed_mm, 1)
            for t in range(ST):
                loose(v.max(chan[:, t, :], keyed_ps[t]))
            dve.wait_ge(routes, 1)
            dve.wait_ge(placed, 1)
            v.tensor_tensor(pair_at[:, :, :], place_ps[:, :, 0:E], routed[:, :, 0:E], ALU.mult).then_inc(pair_at_set, 1)
            loose(v.tensor_tensor(ev_start[:, :, :], place_ps[:, :, E:2 * E], routed[:, :, E:2 * E], ALU.subtract))
            loose(v.tensor_copy(places[:, :, :], place_ps))
            dve.wait_ge(vec, steps[0] - 2)
            for t in range(ST):
                loose(v.tensor_copy(slot_map[:, t, :, PAIRS:PAIRS + JM], chan[:, t, :].unsqueeze(1).to_broadcast([P, E, JM])))
            dve.wait_ge(vec, steps[0] - ST)
            loose(v.tensor_copy(slot_map[:, :, :, PAIRS + JM], ev_start[:, :, :]))

            def make_maps(e):
                for t in range(ST):
                    v.tensor_scalar(from_start[:, t, e, :], place[:, :], ev_start[:, t, e:e + 1], None, ALU.is_ge)
                    ins = v.tensor_scalar(from_end[:, t, e, :], place[:, :], places[:, t, E + e:E + e + 1], -1.0, ALU.is_ge, ALU.mult)
                    if e in (0, E - 1):
                        ins = v.tensor_scalar(slot_map[:, t, e, 0:PAIRS], slot1[:, 0:PAIRS], pair_at[:, t, e:e + 1], None, ALU.is_equal)
                ins.then_inc(maps_set, 1)

            def make_indices(d):
                one = lambda tile: tile[:, d:d + 1]
                dve.wait_ge(mapped, d + 1)
                link(v.tensor_scalar(one(nth), MAP[d][:, PAIRS + JM:PAIRS + JM + 1], -1.0, part[:, 0:1], ALU.mult, ALU.add))
                loose(v.tensor_scalar(one(ev_base), MAP[d][:, INFO - 1:INFO], 2 * d * H - 1 + FAR, None, ALU.add))
                v.scalar_tensor_tensor(nth_chan[:, d, :], eight[:, :], one(nth), MAP[d][:, PAIRS:PAIRS + JM],
                                       ALU.is_equal, ALU.mult, accum_out=one(ev_chan)).then_inc(info_out, 1)
                dve.wait_ge(info_out, d + 1)
                dve.wait_ge(vec, steps[0])
                v.tensor_scalar(one(w1_index), one(ev_chan), one(ev_base), 0.0, ALU.add, ALU.max).then_inc(indexed, 1)

            def split_w2(e):
                dve.wait_ge(w2_hi_set, e + 1)
                if e >= 2:
                    dve.wait_ge(y_ready, e - 1)
                v.tensor_tensor(w2_lo[:, e % 2, :, :], w2_sb[:, e % WR, :, :], w2_hi[:, e % 3, :, :],
                                ALU.subtract).then_inc(w2_lo_set[e], 1)

            def split_h(d):
                for half in range(2):
                    dve.wait_ge(h_done, 4 * d + 2 + half + 1)
                    at = (slice(None), d % 2, slice(half * CH, (half + 1) * CH), slice(None))
                    v.tensor_tensor(hT_lo[at], hT[at], hT_hi[at], ALU.subtract).then_inc(h_lo_set, 1)

            def take_y(e):
                d = e // 2
                dve.wait_ge(y_ready, e + 1)
                if e % 2 == 0:
                    v.tensor_scalar(y_even[:, d % 2, :], Y[0], pair_gate[:, e:e + 1], None, ALU.mult).then_inc(y_set, 1)
                else:
                    dve.wait_ge(y_set, e)
                    v.scalar_tensor_tensor(y[:, d % 2, :], Y[1], pair_gate[:, e:e + 1], y_even[:, d % 2, :],
                                           ALU.mult, ALU.add).then_inc(y_set, 1)

            def split_y(d):
                if d >= 2:
                    dve.wait_ge(combined, ST * (d - 1))
                v.scalar_tensor_tensor(y_hi[:, d % 2, :], Y[1], pair_gate[:, 2 * d + 1:2 * d + 2], y_even[:, d % 2, :],
                                       ALU.mult, ALU.add).then_inc(y_hi_set, 1)
                dve.wait_ge(y_hi_set, d + 1)
                dve.wait_ge(y_set, 2 * d + 2)
                v.tensor_tensor(y_lo[:, d % 2, :], y[:, d % 2, :], y_hi[:, d % 2, :], ALU.subtract).then_inc(y_lo_set, 1)

            make_maps(0)
            make_maps(1)
            make_maps(2)
            loose(v.tensor_tensor(out_index[:, :], token_no[:, :], unused[:, :], ALU.add))
            loose(v.tensor_tensor(top_sum[:, :], best[:, :, 0], best[:, :, 1], ALU.add))
            make_indices(0)
            loose(v.reciprocal(top_inv[:, :], top_sum[:, :]))
            make_maps(3)
            make_maps(4)
            dve.wait_ge(vec, steps[0])
            loose(v.tensor_tensor(gate1[:, :], best[:, :, 0], top_inv[:, :], ALU.mult))
            loose(v.tensor_tensor(gate2[:, :], best[:, :, 1], top_inv[:, :], ALU.mult))
            make_indices(1)
            make_maps(5)
            make_maps(6)
            for k, (dst, gate) in enumerate(((gates_a, gate1), (gates_b, gate2))):
                loose(v.tensor_tensor(dst[:, :, :], kept[:, :, k * E:(k + 1) * E],
                                      gate[:, :].unsqueeze(2).to_broadcast([P, ST, E]), ALU.mult))
            make_indices(2)
            make_maps(7)
            dve.wait_ge(vec, steps[0])
            link(v.tensor_tensor(gates[:, :, :], gates_a[:, :, :], gates_b[:, :, :], ALU.add))
            link(v.tensor_copy(pair_info[:, :, 0, :], gates[:, :, :]))
            link(v.tensor_tensor(gates_r[:, :, :], gates[:, :, :], pair_info[:, :, 0, :], ALU.subtract))
            link(v.tensor_copy(pair_info[:, :, 1, :], gates_r[:, :, :]))
            loose(v.tensor_scalar(pair_info[:, :, 3, :], slot_no[:, :].unsqueeze(2).to_broadcast([P, ST, E]), 1.0, None, ALU.add))
            v.tensor_tensor(pair_info[:, :, 2, :], gates_r[:, :, :], pair_info[:, :, 1, :], ALU.subtract).then_inc(info_set2, 1)
            split_h(0)
            make_indices(3)
            split_w2(1)

            dve.wait_ge(pair_mm, 1)
            link(v.tensor_copy(pairs[:, :, :], pair_ps))
            loose(v.tensor_tensor(pair_slot[:, :], pairs[:, 0::2, 3], pairs[:, 1::2, 3], ALU.add))
            link(v.tensor_tensor(pair_a[:, :], pairs[:, :, 0], pairs[:, :, 1], ALU.add))
            link(v.tensor_tensor(pair_gate[:, :], pair_a[:, :], pairs[:, :, 2], ALU.add))
            take_y(0)

            def map_out_slots(d):
                v.tensor_scalar(to_out[:, d, :], slot1[:, :], pair_slot[:, d:d + 1], None, ALU.is_equal).then_inc(paired, 1)

            split_w2(2)
            split_h(1)
            take_y(1)
            split_y(0)
            for d in range(D):
                map_out_slots(d)
            take_y(2)
            split_w2(4)
            split_h(2)
            C = 1
            link(v.tensor_scalar(in_range[:, :], cond3[:, :], 0.0, None, ALU.is_ge))
            link(v.scalar_tensor_tensor(theta_r[:, :], cond3[:, :], 1.0, in_range[:, :], ALU.is_lt, ALU.mult))
            link(v.tensor_reduce(theta[:, 0:1], theta_r[:, :], AX_X, ALU.add))
            loose(v.tensor_scalar(faults[0:3 * B, C:C + 1], theta[:, 0:1], -1.0, float(H), ALU.mult, ALU.add))
            C += 1
            loose(v.tensor_scalar(faults[:, C:C + 1], before[:, TILES:TILES + 1], -float(SLOTS), None, ALU.add))
            C += 1
            take_y(3)
            split_y(1)
            take_y(4)
            split_w2(6)
            split_h(3)
            take_y(5)
            split_y(2)
            split_w2(7)
            link(v.tensor_scalar(chan_hit[:, :, :], chan[:, :, :], 0.0, None, ALU.is_gt))
            link(v.tensor_reduce(hits[:, :], chan_hit[:, :, :], AX_X, ALU.add))
            loose(v.tensor_tensor(faults[:, C:C + ST], hits[:, :], slot_info[:, :, 2], ALU.not_equal))
            C += ST
            for ends, room in ((0, PAIRS), (E, EVENTS)):
                loose(v.tensor_scalar(faults[:, C:C + ST * E].rearrange("p (t e) -> p t e", t=ST),
                                      places[:, :, ends:ends + E], -float(room), None, ALU.add))
                C += ST * E
            assert C == NV
            dve.wait_ge(x_seen, 1)
            dve.wait_ge(vec, steps[0])
            take_y(6)
            link(v.tensor_scalar(fine[:, :], faults[:, :], 0.0, None, ALU.is_le))
            v.tensor_reduce(fine_sum[:, :], fine[:, :], AX_X, ALU.add).then_inc(summed_up, 1)
            take_y(7)
            dve.wait_ge(verdict_mm, 1)
            link(v.tensor_copy(fine_all[:, :], verdict_ps))
            v.tensor_copy(verdict[:, :], fine_all[:, :]).then_inc(verdict_set, 1)

            dve.wait_ge(added, 16 * ST)
            dve.wait_ge(verdict_set, 1)
            with dve.If(dve.value_load(verdict[0:1, 0:1]) != P * NV):
                dve.sem_inc(g_rates, 1)
                dve.sem_inc(y_add, 1)
                dve.wait_ge(turned, 1)
                setup = [0]

                def set_up(ins):
                    setup[0] += 1
                    ins.then_inc(turned_out, 1)
                    dve.wait_ge(turned_out, setup[0])

                set_up(v.tensor_copy(stateT[:, :, :], bank[0][:, 0:KC * B].rearrange("p (k b) -> p k b", k=KC)))
                set_up(v.tensor_copy(gs_i[:, :, :], stateT[:, :, :]))
                set_up(v.tensor_copy(gs_f[:, :, :], gs_i[:, :, :]))
                set_up(v.tensor_tensor(gs_gt[:, :, :], gs_f[:, :, :], stateT[:, :, :], ALU.is_gt))
                set_up(v.tensor_tensor(floor_stateT[:, :, :], gs_f[:, :, :], gs_gt[:, :, :], ALU.subtract))
                set_up(v.memset(g_seen[:, :], 0.0))
                with dve.Fori(0, TILES) as j:
                    done = [0]

                    def link(ins):
                        done[0] += 1
                        ins.then_inc(g_vec, 1)
                        dve.wait_ge(g_vec, j * V + done[0])

                    one = lambda n: g_one[:, n:n + 1]
                    dve.wait_ge(gx_in, j * 16 + 16)
                    v.tensor_scalar(g_rate[:, :], g_x[:, :], 0.0, float(DT), ALU.max, ALU.mult).then_inc(g_rates, 1)
                    dve.wait_ge(g_cums, j + 1)
                    for k in range(KC):
                        link(v.tensor_tensor(
                            g_c[:, k, :].rearrange("p (b t) -> p b t", b=BPT), csum[:, k, :].rearrange("p (b t) -> p b t", b=BPT),
                            stateT[:, k, bass.ds(j * BPT, BPT)].unsqueeze(2).to_broadcast([P, BPT, T]), ALU.add))
                    link(v.tensor_copy(g_ci[:, :, :], g_c[:, :, :]))
                    link(v.tensor_copy(g_cf[:, :, :], g_ci[:, :, :]))
                    link(v.tensor_tensor(g_gt[:, :, :], g_cf[:, :, :], g_c[:, :, :], ALU.is_gt))
                    link(v.tensor_tensor(g_fl[:, :, :], g_cf[:, :, :], g_gt[:, :, :], ALU.subtract))
                    fl = g_fl[:, :, :].rearrange("p k (b t) -> p (k b) t", b=BPT)
                    spk = g_sp[:, :, :].rearrange("p k (b t) -> p (k b) t", b=BPT)
                    link(v.tensor_tensor(spk[:, :, 1:T], fl[:, :, 1:T], fl[:, :, 0:T - 1], ALU.subtract))
                    for k in range(KC):
                        link(v.tensor_tensor(spk[:, k * BPT:(k + 1) * BPT, 0], fl[:, k * BPT:(k + 1) * BPT, 0],
                                                     floor_stateT[:, k, bass.ds(j * BPT, BPT)], ALU.subtract))
                    v.tensor_scalar(g_xt[:, :, :], g_sp[:, :, :], SPIKE, None, ALU.mult).then_inc(g_xts, 1)
                    dve.wait_ge(g_xts, j + 1)
                    link(v.tensor_copy(g_XT[:, :, bass.ds(j * P, P)], g_xt[:, :, :]))
                    dve.wait_ge(g_logits, j + 1)
                    link(v.tensor_reduce(one(0), logit, AX_X, ALU.max))
                    v.tensor_scalar(one(1), one(0), -1.0, None, ALU.mult).then_inc(g_max, 1)
                    dve.wait_ge(g_exps, j + 1)
                    link(v.tensor_reduce(one(2), g_e[:, :], AX_X, ALU.max))
                    link(v.scalar_tensor_tensor(g_key[:, :], g_e[:, :], one(2), desc[:, :], ALU.is_equal, ALU.mult))
                    link(v.tensor_reduce(one(3), g_key[:, :], AX_X, ALU.max))
                    link(v.tensor_scalar(g_oh[:, 0:E], desc[:, :], one(3), None, ALU.is_equal))
                    link(v.scalar_tensor_tensor(g_e2[:, :], g_oh[:, 0:E], -2.0, g_e[:, :], ALU.mult, ALU.add))
                    link(v.tensor_reduce(one(4), g_e2[:, :], AX_X, ALU.max))
                    link(v.scalar_tensor_tensor(g_key[:, :], g_e2[:, :], one(4), desc[:, :], ALU.is_equal, ALU.mult))
                    link(v.tensor_reduce(one(5), g_key[:, :], AX_X, ALU.max))
                    v.tensor_scalar(g_oh[:, E:2 * E], desc[:, :], one(5), None, ALU.is_equal).then_inc(g_hot, 1)
                    link(v.tensor_tensor(one(6), one(2), one(4), ALU.add))
                    link(v.reciprocal(one(7), one(6)))
                    link(v.tensor_tensor(one(8), one(2), one(7), ALU.mult))
                    link(v.tensor_tensor(one(9), one(4), one(7), ALU.mult))
                    dve.wait_ge(g_ranks, j + 1)
                    dve.wait_ge(g_hot, j + 1)
                    link(v.tensor_tensor(g_rank[:, :], rank_ps, g_seen[:, :], ALU.add))
                    link(v.tensor_tensor(g_seen[:, :], total_ps, g_seen[:, :], ALU.add))
                    link(v.scalar_tensor_tensor(g_kept[:, :], g_rank[:, :], float(CAP), g_oh[:, :], ALU.is_le, ALU.mult))
                    link(v.tensor_scalar(g_tmp[:, :], g_kept[:, 0:E], one(8), None, ALU.mult))
                    link(v.scalar_tensor_tensor(g_gates[:, bass.ds(j * E, E)], g_kept[:, E:2 * E], one(9), g_tmp[:, :], ALU.mult, ALU.add))
                    assert done[0] == V, done
                v.tensor_copy(g_one[:, 10:11], g_one[:, 9:10]).then_inc(g_routed, 1)
                gates3 = g_gates[:, :].rearrange("p (j e) -> p j e", e=E)
                with dve.Fori(0, E) as e:
                    with dve.Fori(0, NQ) as q:
                        step = e * NQ + q
                        dve.wait_ge(y_add, step * GQ + 1)
                        v.tensor_copy(g_gcol[:, :], gates3[:, bass.ds(q * GQ, GQ), bass.ds(e, 1)].rearrange("p a b -> p (a b)")).then_inc(g_routed, 1)
                        dve.wait_ge(g_routed, step + 2)
                        dve.wait_ge(y_mm, step + 2)
                        for s in range(GQ):
                            a = g_acc[:, bass.ds(q * GQ + s, 1), :].rearrange("p a c -> p (a c)")
                            v.scalar_tensor_tensor(a, bank[2 + s][:, 0:H], g_gcol[:, s:s + 1], a, ALU.mult, ALU.add).then_inc(y_add, 1)



_INS = ["x", "cond_1024", "L0_ffn_router_w", "L0_ffn_w1", "L0_ffn_w2"]
_OUTS = [((32, 64, 256), "float32")]


def kernel(**inputs):
    import numpy as _np
    import concourse.bacc as _bacc
    from concourse import mybir as _mybir
    from concourse.bass_utils import run_bass_kernel_spmd as _run

    nc = _bacc.Bacc("TRN2", target_bir_lowering=False, num_devices=1)
    arrays, args = {}, []
    for name in _INS:
        a = _np.ascontiguousarray(inputs[name])
        arrays[f"in_{name}_dram"] = a
        args.append(nc.dram_tensor(f"in_{name}_dram", a.shape, _mybir.dt.from_np(a.dtype), kind="ExternalInput").ap())
    for i, (shape, dtype) in enumerate(_OUTS):
        dt = _mybir.dt.from_np(_np.dtype(dtype))
        args.append(nc.dram_tensor(f"out_{i}_dram", shape, dt, kind="ExternalOutput").ap())
    adaln_ffn_kernel(nc, *args)
    r = _run(nc, [arrays], core_ids=[0])
    return r.results[0]["out_0_dram"]
```
